# Optimizing a Trainium2 kernel written in Bass

```python
import numpy as np
import jax
import jax.numpy as jnp

def _softmax(x, axis=-1):
    return jax.nn.softmax(x, axis=axis)

def _gelu(x):
    return jax.nn.gelu(x, approximate=True)

def _silu(x):
    return jax.nn.silu(x)

def _sigmoid(x):
    return jax.nn.sigmoid(x)

def _layernorm(x, axis=-1, eps=1e-05):
    m = jnp.mean(x, axis=axis, keepdims=True)
    v = jnp.var(x, axis=axis, keepdims=True)
    return (x - m) / jnp.sqrt(v + eps)

def _scatter_add(tgt, idx, src, axis=0):
    return tgt.at[idx].add(src)

def _segment_sum(src, seg, n):
    return jax.ops.segment_sum(src, seg, n)
kernel_name = 'mk_xattn_seq_d2_seqx_r8_d16588'

def setup_inputs(seed: int=0):
    np.random.seed(seed)
    _w = jnp.asarray

    def _rec_inputs():
        import jax
        import jax.numpy as jnp
        _rk = jax.random.key(seed)
        x = -0.0002928 + 1 * jax.random.normal(jax.random.fold_in(_rk, 1), (8, 100, 128), jnp.float32)
        _lenS = 100 - jax.random.randint(jax.random.fold_in(_rk, 7), (8,), 0, max(1, 100 // 4) + 1, jnp.int32)
        _lenS2 = 1444 - jax.random.randint(jax.random.fold_in(_rk, 8), (8,), 0, max(1, 1444 // 4) + 1, jnp.int32)
        _ctx_1024P = jax.random.normal(jax.random.fold_in(_rk, 11), (8, 16, 128), jnp.float32)
        _ctx_1024c = jax.random.dirichlet(jax.random.fold_in(_rk, 511), 0.3 * jnp.ones((16,), jnp.float32), (8, 1444))
        _ctx_1024t = jnp.einsum('bsk,bkd->bsd', _ctx_1024c, _ctx_1024P)
        _ctx_1024t = _ctx_1024t * jax.lax.rsqrt(jnp.mean(jnp.square(_ctx_1024t)) + 1e-12) * 0.953939
        ctx_1024 = -1.39393e-06 + 0.999914 * (_ctx_1024t + 0.3 * jax.random.normal(jax.random.fold_in(_rk, 611), (8, 1444, 128), jnp.float32))
        return (x, ctx_1024)
    x, ctx_1024 = _rec_inputs()

    def _L0_xattn_setup():
        import jax, jax.numpy as jnp
        import numpy as np
        B, Q, KV = (2, 256, 256)
        D_MODEL = 128
        N_HEADS = 16
        D_KV = 64
        EPS = 1e-06
        key = jax.random.key(seed)
        ks = jax.random.split(key, 7)
        s = 0.02
        return {'hidden_states': jax.random.normal(ks[0], (B, Q, D_MODEL), jnp.float32), 'key_value_states': jax.random.normal(ks[1], (B, KV, D_MODEL), jnp.float32), 'wq': jax.random.normal(ks[2], (D_MODEL, N_HEADS * D_KV), jnp.float32) * s, 'wk': jax.random.normal(ks[3], (D_MODEL, N_HEADS * D_KV), jnp.float32) * s, 'wv': jax.random.normal(ks[4], (D_MODEL, N_HEADS * D_KV), jnp.float32) * s, 'wo': jax.random.normal(ks[5], (N_HEADS * D_KV, D_MODEL), jnp.float32) * s, 'norm_w': jnp.ones((D_MODEL,), jnp.float32)}
    _L0_xattn_all = _L0_xattn_setup()
    _L0_xattn_in = {k: v for k, v in _L0_xattn_all.items() if k in ('wq', 'wk', 'wv', 'wo', 'norm_w')}
    del _L0_xattn_all

    def _L1_xattn_setup():
        import jax, jax.numpy as jnp
        import numpy as np
        B, SR, SF, D = (8, 256, 256, 128)
        key = jax.random.key(seed)
        k1, k2 = jax.random.split(key)
        H_real = jax.random.normal(k1, (B, SR, D), dtype=jnp.float32)
        H_fake = jax.random.normal(k2, (B, SF, D), dtype=jnp.float32)
        return {'H_real': H_real, 'H_fake': H_fake}
    _L1_xattn_all = _L1_xattn_setup()
    _L1_xattn_in = {k: v for k, v in _L1_xattn_all.items() if k in ()}
    del _L1_xattn_all
    return {'x': x, 'ctx_1024': ctx_1024, 'L0_xattn_wq': _L0_xattn_in['wq'], 'L0_xattn_wk': _L0_xattn_in['wk'], 'L0_xattn_wv': _L0_xattn_in['wv'], 'L0_xattn_wo': _L0_xattn_in['wo'], 'L0_xattn_norm_w': _L0_xattn_in['norm_w']}

def reference(x, ctx_1024, L0_xattn_wq, L0_xattn_wk, L0_xattn_wv, L0_xattn_wo, L0_xattn_norm_w):
    import jax
    import jax.numpy as jnp

    def _L0_xattn_ref(hidden_states, key_value_states, wq, wk, wv, wo, norm_w):
        import jax, jax.numpy as jnp
        import numpy as np
        B, Q, KV = (2, 256, 256)
        D_MODEL = 128
        N_HEADS = 16
        D_KV = 64
        EPS = 1e-06
        var = jnp.mean(jnp.square(hidden_states), axis=-1, keepdims=True)
        normed = hidden_states * jax.lax.rsqrt(var + EPS) * norm_w
        b, q_len, _ = hidden_states.shape
        kv_len = key_value_states.shape[1]

        def split_heads(x):
            return x.reshape(b, -1, N_HEADS, D_KV).transpose(0, 2, 1, 3)
        q = split_heads(normed @ wq)
        k = split_heads(key_value_states @ wk)
        v = split_heads(key_value_states @ wv)
        scores = jnp.einsum('bhqd,bhkd->bhqk', q, k)
        attn = jax.nn.softmax(scores.astype(jnp.float32), axis=-1).astype(scores.dtype)
        ctx = jnp.einsum('bhqk,bhkd->bhqd', attn, v)
        ctx = ctx.transpose(0, 2, 1, 3).reshape(b, q_len, N_HEADS * D_KV)
        attn_out = ctx @ wo
        return hidden_states + attn_out

    def _L1_xattn_ref(H_real, H_fake):
        import jax, jax.numpy as jnp
        import numpy as np
        B, SR, SF, D = (8, 256, 256, 128)
        scores = jnp.einsum('brd,bfd->brf', H_real, H_fake)
        weights = jax.nn.softmax(scores, axis=-1)
        context = jnp.einsum('brf,bfd->brd', weights, H_fake)
        return H_real + context
    x = _L0_xattn_ref(x, ctx_1024, L0_xattn_wq, L0_xattn_wk, L0_xattn_wv, L0_xattn_wo, L0_xattn_norm_w)
    x = _L1_xattn_ref(x, ctx_1024)
    return x

_drawn_inputs = setup_inputs


def setup_inputs(seed=0):
    import zlib

    import numpy as np

    out = dict(_drawn_inputs(seed))
    spreads = {'L0_xattn_norm_w': (1.0, 0.6)}
    factors = {'L0_xattn_wq': 2.854, 'L0_xattn_wk': 2.956}
    for name, (base, spread) in spreads.items():
        noise = np.random.default_rng([zlib.crc32(name.encode()), seed]).standard_normal(out[name].shape)
        drawn = base * np.exp(spread * noise) if base else spread * noise
        out[name] = jnp.asarray(drawn.astype(out[name].dtype))
    for name, factor in factors.items():
        out[name] = (out[name] * factor).astype(out[name].dtype)
    return out
```

```python
from contextlib import ExitStack

import concourse.bass as bass
from concourse import mybir

F32 = mybir.dt.float32
F32R = mybir.dt.float32r
ALU = mybir.AluOpType
ACT = mybir.ActivationFunctionType
AX = mybir.AxisListType

EPS = 1e-6
DH = 64
P = 128


def bass_two_cross_attentions(nc, x, ctx_in, wq, wk, wv, wo, norm_w, out):
    B, Q, D = x.shape
    S = ctx_in.shape[1]
    H = wq.shape[1] // DH
    HP = H // 2
    R = H * Q
    TM = 124
    NT = -(-R // TM)
    FULL = S // P
    TAIL = S - FULL * P
    SLOTS = FULL + 1
    assert D == P and 3 * TAIL <= P and R % 2 == 0 and B % 2 == 0

    LATE = -1
    ITEMS = [0, 1, 2, 3, 4, 5, 6, 7, LATE, 8, 9, 10, 11, 12]
    STEPS = len(ITEMS)
    LATE_AT = ITEMS.index(LATE)
    CHUNKS = [(0, 512), (512, 512), (1024, S - 1024)]
    NC = len(CHUNKS)
    TILE_SLOTS = [(0, 4), (4, 4), (8, 4)]
    GROUPS = [(0, 1), (2, 3), (4, 5), (6, 7), (8,), (9, 10), (11, 12)]
    NG = len(GROUPS)
    LATE_GROUP, LATE_COL = 4, TM
    GW = 2 * TM

    def rows(item):
        return Q if item == LATE else min(TM, R - TM * item)

    def group_of(item):
        return LATE_GROUP if item == LATE else [g for g in range(NG) if item in GROUPS[g]][0]

    def group_col(item):
        return LATE_COL if item == LATE else TM * GROUPS[group_of(item)].index(item)

    def group_width(g):
        return sum(rows(t) for t in GROUPS[g])

    PV_PLAN = {0: (5, -1, 1, 2), 1: (6, -1, 0, 2), 2: (6, -1, 1, 2),
               3: (0, 0, 0, 2), 4: (0, 0, 1, 2), 5: (1, 0, 0, 2), 6: (1, 0, 1, 2),
               7: (2, 0, 0, 2), 8: (2, 0, 1, 2), 9: (3, 0, 0, 2), 10: (3, 0, 1, 2),
               11: (LATE, -1, 0, 1), 12: (4, 0, 0, 1), 13: (5, 0, 0, 2)}
    PV_PIECES = 2
    PV_LAST = {(g, off): s for s, (g, off, part, parts) in PV_PLAN.items() if part == parts - 1}
    PAIR_STEPS = {1: 0, 6: 1, 7: 2, 8: 3, 9: 4, 10: 5, 13: 6}
    LAST_PAIR_STEP = 0
    OUT_HEADS = {2: range(0, 5), 3: range(5, 9), 4: range(9, 13), 5: range(13, 16)}
    OUT_STEP = max(OUT_HEADS)
    ROW_STEP = 11
    FIN_STEP = 12
    CTX_T_STEPS = [9, 10, 11]
    CTX_SPLIT = [(0, 4), (4, 8), (8, 12)]
    CTX_SPLIT_STEPS = {12: (0, 1), 13: (1, 1), 0: (2, 0)}
    STACK_STEP = 1

    def n(b, per_batch, index):
        return b * per_batch + index + 1

    def need(eng, sem, value):
        if not (isinstance(value, int) and value <= 0):
            eng.wait_ge(sem, value)

    def head_cols(h):
        at = (h % 2) * HP + h // 2
        return slice(P * at, P * (at + 1))

    scratch = nc.dram_tensor("denominator_rows", [B, NT * TM], F32).ap()

    with ExitStack() as stack:
        def sb(name, shape, dt=F32):
            return stack.enter_context(nc.sbuf_tensor(name, shape, dt))

        def sem(name):
            return stack.enter_context(nc.semaphore(name))

        ident = sb("ident", [P, P])
        lo_rows = sb("lo_rows", [P, 1])
        hi_rows = sb("hi_rows", [P, 1])
        norm_col = sb("norm_col", [P, 1])
        x_T = sb("x_T", [P, B * Q])
        xn_hi = sb("xn_hi", [P, B * Q], F32R)
        xn_lo = sb("xn_lo", [P, B * Q], F32R)
        wqk_hi = sb("wqk_hi", [P, H * D], F32R)
        wqk_lo = sb("wqk_lo", [P, H * D], F32R)
        wvo_hi = sb("wvo_hi", [P, H * D], F32R)
        wvo_lo = sb("wvo_lo", [P, H * D], F32R)
        q_hi = sb("q_hi", [P, R], F32R)
        q_lo = sb("q_lo", [P, R], F32R)
        ctx_raw = sb("ctx_raw", [P, SLOTS, D])
        c_hi = [sb(f"c_hi{i}", [P, SLOTS, D], F32R) for i in range(2)]
        c_lo = [sb(f"c_lo{i}", [P, FULL, D], F32R) for i in range(2)]
        cT_hi = [sb(f"cT_hi{i}", [P, S], F32R) for i in range(2)]
        cT_lo = [sb(f"cT_lo{i}", [P, S], F32R) for i in range(2)]
        tail_a = sb("tail_a", [P, D])
        tail_b = sb("tail_b", [P, D])
        probs = [sb(f"probs{i}", [P, S]) for i in range(2)]
        tails = [sb(f"tails{i}", [P, P]) for i in range(2)]
        part_max = sb("part_max", [P, STEPS, NC])
        neg_max = sb("neg_max", [P, STEPS])
        sums = sb("sums", [P, STEPS, NC])
        denom = sb("denom", [P, STEPS])
        rinv = sb("rinv", [P, STEPS])
        rinv_row = sb("rinv_row", [P, 2, GW])
        o_part = sb("o_part", [P, GW])
        o_raw = sb("o_raw", [P, GW])
        o_norm = sb("o_norm", [P, GW])
        o_both = sb("o_both", [P, 2, R], F32R)
        q_part = sb("q_part", [P, 2 * Q])
        q_raw = sb("q_raw", [P, 2 * Q])
        x1_part = sb("x1_part", [P, Q])
        x1_T = sb("x1_T", [P, Q])
        x1_hi = sb("x1_hi", [P, Q], F32R)
        x1_lo = sb("x1_lo", [P, Q], F32R)
        x1_rows = sb("x1_rows", [P, D])
        late_T = sb("late_T", [P, Q])
        result = sb("result", [P, D])
        stats = sb("stats", [P, 6, B])
        wv_sb = sb("wv_sb", [P, H * DH])
        wo_sb = sb("wo_sb", [P, HP, D])
        wvT = sb("wvT", [P, HP * D])
        xb_both = [sb(f"xb_both{i}", [P, 2, Q], F32R) for i in range(2)]

        with ExitStack() as early:
            def tmp(name, shape):
                return early.enter_context(nc.sbuf_tensor(name, shape, F32))
            wq_sb = tmp("wq_sb", [P, H * DH])
            wk_sb = tmp("wk_sb", [P, H * DH])
            wqT = tmp("wqT", [P, HP * D])
            wkT = tmp("wkT", [P, HP * D])
            x_rows = tmp("x_rows", [P, B, D])
            x_sq = tmp("x_sq", [P, B, D])
            xn_rows = tmp("xn_rows", [P, B, D])
        pT_both = [sb(f"pT_both{i}", [P, SLOTS, 2, GW], F32R) for i in range(2)]

        def ps(name, banks):
            return stack.enter_context(nc.psum_tensor(name, [P, banks, 512], F32))

        ps_s = ps("ps_s", 4)
        ps_t = ps("ps_t", 2)
        ps_o = ps("ps_o", 1)
        ps_m = ps("ps_m", 1)

        WVT_BANKS = [ps_o[:, 0], ps_m[:, 0]]
        WVO_PLAN = {1: [(0, ps_o[:, 0])], 2: [(1, ps_m[:, 0]), (2, ps_o[:, 0])], 3: [(3, ps_m[:, 0])]}

        x_loaded = sem("x_loaded")
        wqk_loaded = sem("wqk_loaded")
        wvo_loaded = sem("wvo_loaded")
        norm_loaded = sem("norm_loaded")
        ctx_loaded = sem("ctx_loaded")
        consts_begun = sem("consts_begun")
        consts_ready = sem("consts_ready")
        ident_begun = sem("ident_begun")
        ident_ready = sem("ident_ready")
        x_squared = sem("x_squared")
        x_meansq = sem("x_meansq")
        x_root = sem("x_root")
        x_newton = sem("x_newton")
        xn_ready = sem("xn_ready")
        wT_turned = sem("wT_turned")
        wqT_copied = sem("wqT_copied")
        wkT_copied = sem("wkT_copied")
        wqk_made = sem("wqk_made")
        wqk_hi_done = sem("wqk_hi_done")
        wqk_lo_done = sem("wqk_lo_done")
        x_turned = sem("x_turned")
        xT_copied = sem("xT_copied")
        xn_hi_done = sem("xn_hi_done")
        xn_lo_done = sem("xn_lo_done")
        q0_made = sem("q0_made")
        q0_hi_done = sem("q0_hi_done")
        q0_lo_done = sem("q0_lo_done")
        wvT_turned = sem("wvT_turned")
        wvT_copied = sem("wvT_copied")
        wvo_made = sem("wvo_made")
        wvo_hi_done = sem("wvo_hi_done")
        wvo_lo_done = sem("wvo_lo_done")
        kinds = ("tile", "late")
        scored = {k: sem(f"scored_{k}") for k in kinds}
        chunk_max = {k: sem(f"chunk_max_{k}") for k in kinds}
        maxed = {k: sem(f"maxed_{k}") for k in kinds}
        exped = {k: sem(f"exped_{k}") for k in kinds}
        tail_hi = {k: sem(f"tail_hi_{k}") for k in kinds}
        tail_split = {k: sem(f"tail_split_{k}") for k in kinds}
        turned = {k: sem(f"turned_{k}") for k in kinds}
        turned_hi = {k: sem(f"turned_hi_{k}") for k in kinds}
        turned_lo = {k: sem(f"turned_lo_{k}") for k in kinds}
        denom_sum = {k: sem(f"denom_sum_{k}") for k in kinds}
        inverted = {k: sem(f"inverted_{k}") for k in kinds}
        pv_done = {k: sem(f"pv_done_{k}") for k in kinds}
        pv_part_out = {k: sem(f"pv_part_out_{k}") for k in kinds}
        pv_out = {k: sem(f"pv_out_{k}") for k in kinds}
        ctx_turned = sem("ctx_turned")
        ctxT_hi = sem("ctxT_hi")
        ctxT_lo = sem("ctxT_lo")
        ctx_hi_done = sem("ctx_hi_done")
        ctx_lo_done = sem("ctx_lo_done")
        stack_steps = sem("stack_steps")
        tail_masked = sem("tail_masked")
        rinv_stored = sem("rinv_stored")
        rinv_row_loaded = [sem(f"rinv_row_loaded{g}") for g in range(NG)]
        o_normed = sem("o_normed")
        o_hi_done = sem("o_hi_done")
        o_split = sem("o_split")
        xb_ready = sem("xb_ready")
        q_made = sem("q_made")
        q_part_out = sem("q_part_out")
        q_summed = sem("q_summed")
        q_hi_done = sem("q_hi_done")
        q_lo_done = sem("q_lo_done")
        proj_made = sem("proj_made")
        x1_begun = sem("x1_begun")
        x1_ready = sem("x1_ready")
        x1_hi_done = sem("x1_hi_done")
        x1_split = sem("x1_split")
        x1_turned = sem("x1_turned")
        x1_rows_ready = sem("x1_rows_ready")
        fin_turned = sem("fin_turned")
        fin_ready = sem("fin_ready")
        stored = sem("stored")
        pool_passed = sem("pool_passed")
        sp_passed = sem("sp_passed")

        def item_exists(step, first, last):
            return not first if ITEMS[step] == LATE else not last

        def item_event(b, step, per_item=1, index=0):
            if step < 0:
                b, step = b - 1, step + STEPS
            if ITEMS[step] == LATE:
                return "late", n(b - 1, per_item, index)
            return "tile", n(b, NT * per_item, ITEMS[step] * per_item + index)

        def score_bank(step, c, par):
            return (NC * (STEPS * par + step) + c) % 4

        def score_before(step, c, first, last):
            at = NC * step + c
            while True:
                at -= 4
                s, k = at // NC, at % NC
                if s < 0:
                    return None if first else (s, k)
                if item_exists(s, first, last):
                    return s, k

        def probs_before(step, first, last):
            step -= 2
            while step >= 0 and not item_exists(step, first, last):
                step -= 2
            return None if step < 0 and first else step

        def pair_parts(part):
            return ps_m[:, 0, 0:4 * Q].rearrange("p (h a q) -> p h a q", h=2, a=2)[:, :, part, :]

        TURNS = []
        for s in range(STEPS):
            TURNS += [("item", s - 1, c) for c in range(NC)]
            if s in CTX_T_STEPS:
                TURNS.append(("ctx", s, CTX_T_STEPS.index(s)))

        def turn_exists(at, first, last, nxt):
            what, s, _ = TURNS[at]
            if what == "ctx":
                return nxt
            if s < 0:
                return not first
            return item_exists(s, first, last)

        def turn_bank(what, s, c, par):
            return (len(TURNS) * par + TURNS.index((what, s, c))) % 2

        def turn_before(b, what, s, c, first, last, nxt):
            at = TURNS.index((what, s, c))
            while True:
                at -= 2
                if at < 0:
                    if first:
                        return None
                    _, s2, c2 = TURNS[at % len(TURNS)]
                    k, v = item_event(b - 1, s2, NC, c2)
                    return turned_lo[k], v
                if turn_exists(at, first, last, nxt):
                    what2, s2, c2 = TURNS[at]
                    if what2 == "ctx":
                        return ctxT_lo, n(b + 1, NC, c2)
                    k, v = item_event(b, s2, NC, c2)
                    return turned_lo[k], v

        def group_buffer(item, par):
            return (NG * par + group_of(item)) % 2

        def pv_before_group(b, item):
            return n(b, NG, group_of(item) - 2)

        def batch_of_item(b, step):
            return b - 1 if step < 0 or ITEMS[step] == LATE else b

        def groups_finished(s, first, last):
            for (g, off), at in PV_LAST.items():
                if (at + 1) % STEPS == s:
                    off -= at + 1 == STEPS
                    if not (first if off < 0 else last):
                        yield g, off

        def pair_exists(s, first, last, nxt):
            return (s in PAIR_STEPS and nxt) or (s == LAST_PAIR_STEP and not first and not last)

        def pair_at(s):
            return (PAIR_STEPS[s], 0) if s in PAIR_STEPS else (HP - 1, -1)

        def windows(eng, body):
            body(eng, 0, 0, True, False, True)
            with eng.Fori(0, (B - 2) // 2) as i:
                body(eng, i * 2 + 1, 1, False, False, True)
                body(eng, i * 2 + 2, 0, False, False, True)
            body(eng, B - 1, 1, False, False, False)
            body(eng, B, 0, False, True, False)

        block = stack.enter_context(nc.Block())

        @block.sync
        def _(sp):
            def load_ctx(b):
                main = ctx_in[bass.ds(b, 1), 0:FULL * P, :].rearrange("a (p j) d -> p (a j) d", j=FULL)
                sp.dma_start(ctx_raw[:, 0:FULL, :], main).then_inc(ctx_loaded, 16)
                for k in range(3):
                    sp.dma_start(ctx_raw[k * TAIL:(k + 1) * TAIL, FULL, :],
                                 ctx_in[bass.ds(b, 1), FULL * P:S, :].rearrange("a t d -> (a t) d"))\
                        .then_inc(ctx_loaded, 16)

            sp.dma_start(x_rows[0:Q, :, :], x.rearrange("b q d -> q b d")).then_inc(x_loaded, 16)
            sp.dma_start(wq_sb[:, :], wq).then_inc(wqk_loaded, 16)
            sp.dma_start(wk_sb[:, :], wk).then_inc(wqk_loaded, 16)
            sp.dma_start(norm_col[:, :], norm_w.rearrange("(d a) -> d a", a=1)).then_inc(norm_loaded, 16)
            sp.wait_ge(consts_begun, 1)
            load_ctx(0)
            sp.dma_start(wv_sb[:, :], wv).then_inc(wvo_loaded, 16)
            sp.dma_start(wo_sb[:, :, :], wo.rearrange("(g e) d -> e g d", e=P)).then_inc(wvo_loaded, 16)

            def carry():
                sp.sem_inc(sp_passed, 1)

            def window(sp, b, par, first, last, nxt):
                if nxt:
                    sp.wait_ge(ctx_turned, n(b, NC, NC - 1))
                    sp.wait_ge(ctx_lo_done, n(b, len(CTX_SPLIT), len(CTX_SPLIT) - 1))
                    sp.wait_ge(stack_steps, n(b, 3, 2))
                    carry()
                    load_ctx(b + 1)
                for g in range(NG):
                    if not last:
                        t0, k = GROUPS[g][0], len(GROUPS[g])
                        s0 = ITEMS.index(t0)
                        cols = slice(TM * t0, TM * (t0 + k))
                        if g == NG - 1 and not first:
                            sp.wait_ge(stored, n(b - 1, 1, 0) * 16)
                            carry()
                        sp.wait_ge(inverted["tile"], n(b, NG, g))
                        carry()
                        sp.dma_start(scratch[bass.ds(b, 1), cols].rearrange("a (t p) -> p (a t)", p=TM),
                                     rinv[0:TM, s0:s0 + k],
                                     allow_slow_non_contiguous=True).then_inc(rinv_stored, 16)
                        sp.wait_ge(rinv_stored, n(b, NG, g) * 16)
                        carry()
                        need(sp, o_normed, n(b, NG, g - 2))
                        carry()
                        row = scratch[bass.ds(b, 1), cols]
                        sp.dma_start(rinv_row[:, (NG * par + g) % 2, 0:TM * k], row.to_broadcast([P, TM * k]))\
                            .then_inc(rinv_row_loaded[g], 16)
                    if g == NG - 2 and not first:
                        sp.wait_ge(fin_ready, n(b - 1, 1, 0))
                        carry()
                        sp.dma_start(out[bass.ds(b - 1, 1), :, :].rearrange("a q d -> (a q) d"),
                                     result[0:Q, :]).then_inc(stored, 16)

            windows(sp, window)
            sp.wait_ge(stored, 16 * B)

        @block.gpsimd
        def _(pool):
            pool.memset(ident[:, :], 0.0).then_inc(ident_begun, 1)
            pool.wait_ge(ident_begun, 1)
            pool.affine_select(out=ident[:, :], in_=ident[:, :], compare_op=ALU.not_equal, fill=1.0,
                               base=0, pattern=[[-1, P]], channel_multiplier=1).then_inc(ident_ready, 1)
            pool.memset(ctx_raw[:, FULL, :], 0.0).then_inc(consts_begun, 1)
            pool.memset(lo_rows[:, :], 1.0).then_inc(consts_begun, 1)
            for i in range(2):
                pool.memset(tails[i][:, :], 0.0).then_inc(consts_begun, 1)
            pool.memset(sums[:, :, :], 1.0).then_inc(consts_begun, 1)
            pool.wait_ge(consts_begun, 5)
            pool.affine_select(out=lo_rows[:, :], in_=lo_rows[:, :], compare_op=ALU.is_ge, fill=0.0,
                               base=-TAIL, pattern=[[0, 1]], channel_multiplier=1).then_inc(consts_ready, 1)
            pool.wait_ge(consts_ready, 1)
            pool.affine_select(out=lo_rows[:, :], in_=lo_rows[:, :], compare_op=ALU.is_ge, fill=0.0,
                               base=2 * TAIL - 1, pattern=[[0, 1]], channel_multiplier=-1).then_inc(consts_ready, 1)
            pool.wait_ge(consts_ready, 2)
            pool.tensor_scalar(hi_rows[:, :], lo_rows[:, :], -1.0, 1.0, ALU.mult, ALU.add)\
                .then_inc(consts_ready, 1)
            pool.wait_ge(consts_ready, 3)

            def carry():
                pool.sem_inc(pool_passed, 1)

            def split_ctx(b, par, part):
                lo, hi = CTX_SPLIT[part]
                top = min(hi, FULL)
                parts = len(CTX_SPLIT)
                src = ctx_raw[:, lo:top, :]
                pool.wait_ge(ctx_hi_done, n(b, parts, part))
                pool.tensor_tensor(c_lo[par][:, lo:top, :], src, c_hi[par][:, lo:top, :].bitcast(F32),
                                   ALU.subtract).then_inc(ctx_lo_done, 1)

            def stack_tail(b, par):
                raw = ctx_raw[:, FULL, :]
                carry()
                pool.tensor_copy(tail_a[:, :].bitcast(F32R), raw).then_inc(stack_steps, 1)
                pool.wait_ge(stack_steps, n(b, 3, 0))
                pool.tensor_tensor(tail_b[:, :], raw, tail_a[:, :], ALU.subtract).then_inc(stack_steps, 1)
                pool.wait_ge(stack_steps, n(b, 3, 1))
                carry()
                pool.tensor_scalar(tail_a[:, :], tail_a[:, :], hi_rows[:, 0:1], None, ALU.mult)\
                    .then_inc(tail_masked, 1)
                pool.tensor_scalar(tail_b[:, :], tail_b[:, :], lo_rows[:, 0:1], None, ALU.mult)\
                    .then_inc(tail_masked, 1)
                pool.wait_ge(tail_masked, n(b, 2, 1))
                pool.tensor_tensor(c_hi[par][:, FULL, :], tail_a[:, :], tail_b[:, :], ALU.add)\
                    .then_inc(stack_steps, 1)

            pool.wait_ge(ctx_loaded, 16 * 4)
            stack_tail(0, 0)
            for part in range(len(CTX_SPLIT)):
                split_ctx(0, 0, part)

            def window(pool, b, par, first, last, nxt):
                for s in range(STEPS):
                    if s == 0 and nxt:
                        cols = bass.ds((b + 1) * Q, Q)
                        pool.tensor_copy(xb_both[1 - par][:, 0, :], xn_hi[:, cols]).then_inc(xb_ready, 1)
                        pool.tensor_copy(xb_both[1 - par][:, 1, :], xn_lo[:, cols]).then_inc(xb_ready, 1)
                    for g, off2 in groups_finished(s, first, last):
                        if g == LATE:
                            continue
                        bb = b + off2
                        w = group_width(g)
                        cols = slice(TM * GROUPS[g][0], TM * GROUPS[g][0] + w)
                        o_hi, o_lo = o_both[:, 0, cols], o_both[:, 1, cols]
                        pool.wait_ge(rinv_row_loaded[g], n(bb, 1, 0) * 16)
                        pool.wait_ge(pv_out["tile"], n(bb, NG, g))
                        need(pool, o_split, n(bb, NG, g) - 1)
                        pool.tensor_tensor(o_norm[:, 0:w], o_raw[:, 0:w],
                                           rinv_row[:, (NG * ((par + off2) % 2) + g) % 2, 0:w], ALU.mult)\
                            .then_inc(o_normed, 1)
                        pool.wait_ge(o_normed, n(bb, NG, g))
                        if g == 0:
                            need(pool, proj_made, n(bb - 1, 1, 0))
                        carry()
                        pool.tensor_copy(o_hi, o_norm[:, 0:w]).then_inc(o_hi_done, 1)
                        pool.wait_ge(o_hi_done, n(bb, NG, g))
                        pool.tensor_tensor(o_lo, o_norm[:, 0:w], o_hi.bitcast(F32), ALU.subtract)\
                            .then_inc(o_split, 1)
                    if item_exists(s, first, last):
                        item = ITEMS[s]
                        m = rows(item)
                        kind, k = item_event(b, s, NC, NC - 1)
                        pool.wait_ge(exped[kind], k)
                        before = probs_before(s, first, last)
                        if before is not None:
                            kind2, k2 = item_event(b, before, NC, NC - 1)
                            pool.wait_ge(turned[kind2], k2)
                        t = tails[s % 2]
                        src = probs[s % 2][0:m, FULL * P:S]
                        carry()
                        for c in range(2):
                            pool.tensor_copy(t[0:m, c * TAIL:(c + 1) * TAIL].bitcast(F32R), src)\
                                .then_inc(tail_hi[kind], 1)
                        _, k = item_event(b, s, 2, 1)
                        pool.wait_ge(tail_hi[kind], k)
                        pool.tensor_tensor(t[0:m, 2 * TAIL:3 * TAIL].bitcast(F32R), src, t[0:m, 0:TAIL],
                                           ALU.subtract).then_inc(tail_split[kind], 1)
                    if pair_exists(s, first, last, nxt):
                        j, off = pair_at(s)
                        cols = slice(2 * Q * j, 2 * Q * (j + 1))
                        pool.wait_ge(q_summed, n(b + off, HP, j))
                        last_tile = -(-2 * Q * (j + 1) // TM) - 1
                        if off == 0:
                            pool.wait_ge(scored["tile"], n(b, NT * NC, last_tile * NC + NC - 1))
                        else:
                            pool.wait_ge(scored["tile"], n(b - 1, NT * NC, last_tile * NC + NC - 1))
                        carry()
                        pool.tensor_copy(q_hi[:, cols], q_raw[:, :]).then_inc(q_hi_done, 1)
                        pool.wait_ge(q_hi_done, n(b + off, HP, j))
                        pool.tensor_tensor(q_lo[:, cols], q_raw[:, :], q_hi[:, cols].bitcast(F32),
                                           ALU.subtract).then_inc(q_lo_done, 1)
                    if s == OUT_STEP and not first:
                        pool.wait_ge(x1_ready, n(b - 1, 1, 0))
                        carry()
                        pool.tensor_copy(x1_hi[:, :], x1_T[:, :]).then_inc(x1_hi_done, 1)
                        pool.wait_ge(x1_hi_done, n(b - 1, 1, 0))
                        pool.tensor_tensor(x1_lo[:, :], x1_T[:, :], x1_hi[:, :].bitcast(F32),
                                           ALU.subtract).then_inc(x1_split, 1)
                    if s in CTX_SPLIT_STEPS:
                        part, off = CTX_SPLIT_STEPS[s]
                        if nxt if off else not (first or last):
                            split_ctx(b + off, (par + off) % 2, part)
                    if s == STACK_STEP and not (first or last):
                        stack_tail(b, par)

            windows(pool, window)

        @block.scalar
        def _(act):
            act.wait_ge(x_meansq, 2)
            act.activation(stats[0:Q, 2, :], stats[0:Q, 1, :], ACT.Sqrt).then_inc(x_root, 1)
            for i in range(2):
                act.wait_ge(wT_turned, i + 1)
                act.activation(wqT[:, 512 * i:512 * (i + 1)], ps_t[:, i, :], ACT.Copy).then_inc(wqT_copied, 1)
            act.wait_ge(norm_loaded, 16)
            for i in range(4):
                act.wait_ge(wqk_made, i + 1)
                act.activation(wqk_hi[:, 512 * i:512 * (i + 1)], ps_s[:, i, :], ACT.Copy,
                               scale=norm_col[:, 0:1]).then_inc(wqk_hi_done, 1)
            for i in range(2):
                act.wait_ge(x_turned, i + 1)
                act.activation(x_T[:, 400 * i:400 * (i + 1)], ps_t[:, i, 0:400], ACT.Copy).then_inc(xT_copied, 1)
            for i in range(2):
                act.wait_ge(x_turned, i + 3)
                act.activation(xn_hi[:, 400 * i:400 * (i + 1)], (ps_o, ps_m)[i][:, 0, 0:400], ACT.Copy)\
                    .then_inc(xn_hi_done, 1)
            for c, (c0, w) in enumerate(CHUNKS):
                act.wait_ge(ctx_turned, c + 1)
                act.activation(cT_hi[0][:, c0:c0 + w], (ps_t[:, 0], ps_t[:, 1], ps_o[:, 0])[c][:, 0:w], ACT.Copy)\
                    .then_inc(ctxT_hi, 1)
            for i in range(4):
                act.wait_ge(q0_made, i + 1)
                act.activation(q_hi[:, 400 * i:400 * (i + 1)], ps_s[:, i, 0:400], ACT.Copy).then_inc(q0_hi_done, 1)

            def ctx_hi(b, par, part):
                lo, hi = CTX_SPLIT[part]
                top = min(hi, FULL)
                act.activation(c_hi[par][:, lo:top, :], ctx_raw[:, lo:top, :], ACT.Copy).then_inc(ctx_hi_done, 1)

            for part in range(len(CTX_SPLIT)):
                ctx_hi(0, 0, part)
            act.wait_ge(x_turned, 4)
            act.wait_ge(consts_ready, 3)

            def window(act, b, par, first, last, nxt):
                def turned_ctx_hi(s):
                    if not (s in CTX_T_STEPS and nxt):
                        return
                    c = CTX_T_STEPS.index(s)
                    c0, w = CHUNKS[c]
                    act.wait_ge(ctx_turned, n(b + 1, NC, c))
                    if c == 0 and not first:
                        act.wait_ge(scored["late"], n(b - 1, NC, NC - 1))
                    act.activation(cT_hi[1 - par][:, c0:c0 + w],
                                   ps_t[:, turn_bank("ctx", s, c, par), 0:w], ACT.Copy).then_inc(ctxT_hi, 1)

                for s in range(STEPS):
                    for g, off2 in groups_finished(s, first, last):
                        kind = "late" if g == LATE else "tile"
                        w = Q if g == LATE else group_width(g)
                        act.wait_ge(pv_done[kind], n(b - 1, 1, 0) if g == LATE else n(b + off2, NG, g))
                        act.activation(o_part[:, 0:w], ps_o[:, 0, w:2 * w], ACT.Copy)\
                            .then_inc(pv_part_out[kind], 1)
                    prev = s - 1
                    if (prev < 0 and not first) or (prev >= 0 and item_exists(prev, first, last)):
                        item = ITEMS[prev]
                        m, col = rows(item), group_col(item)
                        pb = 1 - par if prev < 0 else par
                        buf = group_buffer(item, pb)
                        bank_par = par
                        wb = b - 1 if prev < 0 else b
                        for c, (j0, nj) in enumerate(TILE_SLOTS):
                            kind, k = item_event(b, prev, NC, c)
                            act.wait_ge(turned[kind], k)
                            if c == 0:
                                need(act, pv_done["tile"], pv_before_group(wb, item) - (LATE_GROUP if last and item == LATE else 0))
                                if group_of(item) == LATE_GROUP + 2:
                                    if isinstance(wb, int) and wb == 0:
                                        pass
                                    else:
                                        act.wait_ge(pv_done["late"], n(wb - 1, 1, 0))
                            bank = turn_bank("item", prev, c, bank_par)
                            act.activation(pT_both[buf][:, j0:j0 + nj, 0, col:col + m],
                                           ps_t[:, bank, 0:nj * m].rearrange("p (j m) -> p j m", m=m),
                                           ACT.Copy).then_inc(turned_hi[kind], 1)
                    if first and s == 0:
                        for i in range(2):
                            act.wait_ge(wvT_turned, i + 1)
                            act.activation(wvT[:, 512 * i:512 * (i + 1)], WVT_BANKS[i], ACT.Copy)\
                                .then_inc(wvT_copied, 1)
                    if item_exists(s, first, last):
                        m = rows(ITEMS[s])
                        kind, k = item_event(b, s)
                        act.wait_ge(maxed[kind], k)
                        before = probs_before(s, first, last)
                        for c, (c0, w) in enumerate(CHUNKS):
                            if before is not None:
                                kind2, k2 = item_event(b, before, NC, c)
                                act.wait_ge(turned[kind2], k2)
                            act.activation(probs[s % 2][0:m, c0:c0 + w],
                                           ps_s[0:m, score_bank(s, c, par), 0:w], ACT.Exp,
                                           bias=neg_max[0:m, s:s + 1],
                                           accum_out=sums[0:m, s, c:c + 1]).then_inc(exped[kind], 1)
                            if c == 1:
                                turned_ctx_hi(s)
                    if s in CTX_SPLIT_STEPS:
                        part, off = CTX_SPLIT_STEPS[s]
                        if nxt if off else not (first or last):
                            if part == 0:
                                act.wait_ge(ctx_loaded, n(b + 1, 1, 0) * 64)
                                if not first:
                                    act.wait_ge(pv_done["late"], n(b - 1, 1, 0))
                            ctx_hi(b + off, (par + off) % 2, part)
                    if first and s in WVO_PLAN:
                        for i, bank in WVO_PLAN[s]:
                            act.wait_ge(wvo_made, i + 1)
                            act.activation(wvo_hi[:, 512 * i:512 * (i + 1)], bank, ACT.Copy)\
                                .then_inc(wvo_hi_done, 1)
                    if pair_exists(s, first, last, nxt):
                        j, off = pair_at(s)
                        act.wait_ge(q_made, n(b + off, HP, j))
                        act.activation(q_part[:, :].rearrange("p (h q) -> p h q", h=2), pair_parts(1), ACT.Copy)\
                            .then_inc(q_part_out, 1)

            windows(act, window)

        @block.vector
        def _(dve):
            dve.wait_ge(x_loaded, 16)
            dve.tensor_tensor(x_sq[0:Q, :, :], x_rows[0:Q, :, :], x_rows[0:Q, :, :], ALU.mult)\
                .then_inc(x_squared, 1)
            dve.wait_ge(x_squared, 1)
            dve.tensor_reduce(stats[0:Q, 0, :], x_sq[0:Q, :, :], AX.X, ALU.add).then_inc(x_meansq, 1)
            dve.wait_ge(x_meansq, 1)
            dve.tensor_scalar(stats[0:Q, 1, :], stats[0:Q, 0, :], 1.0 / D, EPS, ALU.mult, ALU.add)\
                .then_inc(x_meansq, 1)
            dve.wait_ge(x_root, 1)
            dve.reciprocal(stats[0:Q, 3, :], stats[0:Q, 2, :]).then_inc(x_newton, 1)
            dve.wait_ge(x_newton, 1)
            dve.tensor_tensor(stats[0:Q, 4, :], stats[0:Q, 3, :], stats[0:Q, 3, :], ALU.mult)\
                .then_inc(x_newton, 1)
            dve.wait_ge(x_newton, 2)
            dve.tensor_tensor(stats[0:Q, 5, :], stats[0:Q, 4, :], stats[0:Q, 1, :], ALU.mult)\
                .then_inc(x_newton, 1)
            dve.wait_ge(x_newton, 3)
            dve.tensor_scalar(stats[0:Q, 4, :], stats[0:Q, 5, :], -0.5, 1.5, ALU.mult, ALU.add)\
                .then_inc(x_newton, 1)
            dve.wait_ge(x_newton, 4)
            dve.tensor_tensor(stats[0:Q, 5, :], stats[0:Q, 4, :], stats[0:Q, 3, :], ALU.mult)\
                .then_inc(x_newton, 1)
            dve.wait_ge(x_newton, 5)
            for i in range(B):
                dve.tensor_scalar(xn_rows[0:Q, i, :], x_rows[0:Q, i, :], stats[0:Q, 5, i:i + 1], None,
                                  ALU.mult).then_inc(xn_ready, 1)
            for i in range(2):
                dve.wait_ge(wT_turned, i + 3)
                dve.tensor_copy(wkT[:, 512 * i:512 * (i + 1)], (ps_o, ps_m)[i][:, 0, :]).then_inc(wkT_copied, 1)
            dve.wait_ge(norm_loaded, 16)
            for i in range(4):
                dve.wait_ge(wqk_hi_done, i + 1)
                dve.scalar_tensor_tensor(out=wqk_lo[:, 512 * i:512 * (i + 1)], in0=ps_s[:, i, :],
                                         scalar=norm_col[:, 0:1],
                                         in1=wqk_hi[:, 512 * i:512 * (i + 1)].bitcast(F32),
                                         op0=ALU.mult, op1=ALU.subtract).then_inc(wqk_lo_done, 1)

            def lo_part(dst, src, hi, done):
                dve.tensor_tensor(dst, src, hi.bitcast(F32), ALU.subtract).then_inc(done, 1)

            for i in range(2):
                cols = slice(400 * i, 400 * (i + 1))
                dve.wait_ge(xn_hi_done, i + 1)
                lo_part(xn_lo[:, cols], (ps_o, ps_m)[i][:, 0, 0:400], xn_hi[:, cols], xn_lo_done)
            for c, (c0, w) in enumerate(CHUNKS):
                dve.wait_ge(ctxT_hi, c + 1)
                lo_part(cT_lo[0][:, c0:c0 + w], (ps_t[:, 0], ps_t[:, 1], ps_o[:, 0])[c][:, 0:w],
                        cT_hi[0][:, c0:c0 + w], ctxT_lo)
            for i in range(4):
                cols = slice(400 * i, 400 * (i + 1))
                dve.wait_ge(q0_hi_done, i + 1)
                lo_part(q_lo[:, cols], ps_s[:, i, 0:400], q_hi[:, cols], q0_lo_done)
            def invert(b, steps, kind, per, index, m):
                k, v = item_event(b, steps[-1], NC, NC - 1)
                dve.wait_ge(exped[k], v)
                lo, hi = steps[0], steps[-1] + 1
                dve.tensor_reduce(denom[0:m, lo:hi], sums[0:m, lo:hi, :], AX.X, ALU.add)\
                    .then_inc(denom_sum[kind], 1)
                dve.wait_ge(denom_sum[kind], n(b, per, index))
                dve.reciprocal(rinv[0:m, lo:hi], denom[0:m, lo:hi]).then_inc(inverted[kind], 1)

            def window(dve, b, par, first, last, nxt):
                for s in range(STEPS):
                    for g, off2 in groups_finished(s, first, last):
                        if g == LATE:
                            dve.wait_ge(pv_part_out["late"], n(b - 1, 1, 0))
                            dve.tensor_tensor(late_T[:, :], ps_o[:, 0, 0:Q], o_part[:, 0:Q], ALU.add)\
                                .then_inc(pv_out["late"], 1)
                        else:
                            w = group_width(g)
                            dve.wait_ge(pv_part_out["tile"], n(b + off2, NG, g))
                            need(dve, o_normed, n(b + off2, NG, g) - 1)
                            dve.tensor_tensor(o_raw[:, 0:w], ps_o[:, 0, 0:w], o_part[:, 0:w], ALU.add)\
                                .then_inc(pv_out["tile"], 1)

                    here = item_exists(s, first, last)
                    prev = s - 1
                    there = (prev < 0 and not first) or (prev >= 0 and item_exists(prev, first, last))

                    def chunk_maximum(c):
                        if not here:
                            return
                        m = rows(ITEMS[s])
                        kind, k = item_event(b, s, NC, c)
                        dve.wait_ge(scored[kind], k)
                        mx = dve.tensor_reduce(part_max[0:m, s, c:c + 1],
                                               ps_s[0:m, score_bank(s, c, par), 0:CHUNKS[c][1]],
                                               AX.X, ALU.max)
                        if c == NC - 1:
                            mx.then_inc(chunk_max[kind], 1)
                            kind, k = item_event(b, s)
                            dve.wait_ge(chunk_max[kind], k)
                            dve.tensor_reduce(neg_max[0:m, s:s + 1], part_max[0:m, s, :], AX.X, ALU.max,
                                              negate=True).then_inc(maxed[kind], 1)

                    def turned_chunk_lo(c):
                        if not there:
                            return
                        item = ITEMS[prev]
                        m, col = rows(item), group_col(item)
                        buf = group_buffer(item, 1 - par if prev < 0 else par)
                        kind, k = item_event(b, prev, NC, c)
                        dve.wait_ge(turned_hi[kind], k)
                        j0, nj = TILE_SLOTS[c]
                        nj = min(nj, FULL - j0)
                        bank = turn_bank("item", prev, c, par)
                        lo_part(pT_both[buf][:, j0:j0 + nj, 1, col:col + m],
                                ps_t[:, bank, 0:nj * m].rearrange("p (j m) -> p j m", m=m),
                                pT_both[buf][:, j0:j0 + nj, 0, col:col + m], turned_lo[kind])

                    chunk_maximum(0)
                    turned_chunk_lo(0)
                    chunk_maximum(1)
                    chunk_maximum(2)
                    turned_chunk_lo(1)
                    turned_chunk_lo(2)

                    if s in CTX_T_STEPS and nxt:
                        c = CTX_T_STEPS.index(s)
                        c0, w = CHUNKS[c]
                        dve.wait_ge(ctxT_hi, n(b + 1, NC, c))
                        lo_part(cT_lo[1 - par][:, c0:c0 + w], ps_t[:, turn_bank("ctx", s, c, par), 0:w],
                                cT_hi[1 - par][:, c0:c0 + w], ctxT_lo)
                    if first and s in WVO_PLAN:
                        for i, bank in WVO_PLAN[s]:
                            cols = slice(512 * i, 512 * (i + 1))
                            dve.wait_ge(wvo_hi_done, i + 1)
                            lo_part(wvo_lo[:, cols], bank, wvo_hi[:, cols], wvo_lo_done)
                    if pair_exists(s, first, last, nxt):
                        j, off = pair_at(s)
                        dve.wait_ge(q_part_out, n(b + off, HP, j))
                        need(dve, q_lo_done, n(b + off, HP, j) - 1)
                        dve.tensor_tensor(q_raw[:, :].rearrange("p (h q) -> p h q", h=2), pair_parts(0),
                                          q_part[:, :].rearrange("p (h q) -> p h q", h=2), ALU.add)\
                            .then_inc(q_summed, 1)
                    if s == OUT_STEP and not first:
                        dve.wait_ge(proj_made, n(b - 1, 1, 0))
                        dve.wait_ge(xT_copied, 2)
                        dve.tensor_tensor(x1_part[:, :], ps_m[:, 0, 0:Q], x_T[:, bass.ds((b - 1) * Q, Q)],
                                          ALU.add).then_inc(x1_begun, 1)
                        dve.wait_ge(x1_begun, n(b - 1, 1, 0))
                        dve.tensor_tensor(x1_T[:, :], ps_m[:, 0, Q:2 * Q], x1_part[:, :], ALU.add)\
                            .then_inc(x1_ready, 1)
                    if s == ROW_STEP and not first:
                        dve.wait_ge(x1_turned, n(b - 1, 1, 0))
                        if last:
                            dve.wait_ge(fin_ready, n(b - 2, 1, 0))
                        dve.tensor_copy(x1_rows[0:Q, :], ps_m[0:Q, 0, 0:D]).then_inc(x1_rows_ready, 1)
                    if s == FIN_STEP and not first:
                        dve.wait_ge(fin_turned, n(b - 1, 1, 0))
                        dve.wait_ge(inverted["late"], n(b - 1, 1, 0))
                        dve.wait_ge(x1_rows_ready, n(b - 1, 1, 0))
                        dve.scalar_tensor_tensor(out=result[0:Q, :], in0=ps_m[0:Q, 0, 0:D],
                                                 scalar=rinv[0:Q, LATE_AT:LATE_AT + 1],
                                                 in1=x1_rows[0:Q, :], op0=ALU.mult, op1=ALU.add)\
                            .then_inc(fin_ready, 1)
                    if prev < 0:
                        if not first:
                            invert(b - 1, [12, 13], "tile", NG, NG - 1, TM)
                    elif there:
                        if ITEMS[prev] == LATE:
                            k, v = item_event(b, prev, NC, NC - 1)
                            dve.wait_ge(exped[k], v)
                            dve.tensor_reduce(denom[0:Q, prev:prev + 1], sums[0:Q, prev, :], AX.X, ALU.add)\
                                .then_inc(denom_sum["late"], 1)
                            dve.wait_ge(denom_sum["late"], n(b - 1, 1, 0))
                            dve.reciprocal(rinv[0:Q, prev:prev + 1], denom[0:Q, prev:prev + 1])\
                                .then_inc(inverted["late"], 1)
                        else:
                            g = group_of(ITEMS[prev])
                            if ITEMS[prev] == GROUPS[g][-1]:
                                invert(b, [ITEMS.index(t) for t in GROUPS[g]], "tile", NG, g, TM)

            windows(dve, window)

        @block.tensor
        def _(pe):
            def three_pass(dst, a_hi, a_lo, b_hi, b_lo, start=True, stop=True):
                pe.matmul(dst, a_hi, b_hi, start=start, stop=False)
                pe.matmul(dst, a_hi, b_lo, start=False, stop=False)
                return pe.matmul(dst, a_lo, b_hi, start=False, stop=stop)

            def three_pass_pair(bank, c0, w, a_hi, a_lo, b_both, start=True, stop=True):
                pe.matmul(bank[:, c0:c0 + 2 * w].rearrange("p (a w) -> p a w", a=2), a_hi, b_both,
                          start=start, stop=False)
                return pe.matmul(bank[:, c0:c0 + w], a_lo, b_both[:, 0, :], start=False, stop=stop)

            pe.wait_ge(ident_ready, 1)
            pe.wait_ge(wqk_loaded, 32)
            for src, banks in ((wq_sb, (ps_t[:, 0], ps_t[:, 1])), (wk_sb, (ps_o[:, 0], ps_m[:, 0]))):
                for i in range(2):
                    for j in range(4):
                        g = 4 * i + j
                        t = pe.transpose(banks[i][:, P * j:P * (j + 1)], src[:, P * g:P * (g + 1)], ident[:, :])
                    t.then_inc(wT_turned, 1)
            for i in range(4):
                if i < 2:
                    pe.wait_ge(wqT_copied, i + 1)
                    pe.wait_ge(wkT_copied, i + 1)
                for j in range(4):
                    h = 2 * (4 * (i % 2) + j) + i // 2
                    at = slice(DH * (h % 2), DH * (h % 2) + DH)
                    blk = slice(P * (h // 2), P * (h // 2) + P)
                    t = pe.matmul(ps_s[:, i, P * j:P * (j + 1)], wqT[at, blk], wkT[at, blk],
                                  start=True, stop=True)
                t.then_inc(wqk_made, 1)
            pe.wait_ge(xn_ready, B)
            pe.wait_ge(wqT_copied, 2)
            pe.wait_ge(wkT_copied, 2)
            for src, banks in ((x_rows, (ps_t[:, 0], ps_t[:, 1])), (xn_rows, (ps_o[:, 0], ps_m[:, 0]))):
                for i in range(2):
                    for j in range(4):
                        t = pe.transpose(banks[i][:, Q * j:Q * (j + 1)], src[0:Q, 4 * i + j, :],
                                         ident[0:Q, 0:Q])
                    t.then_inc(x_turned, 1)

            def turn_ctx(dst, c):
                j0 = TILE_SLOTS[c][0]
                for j in range(j0, min(j0 + 4, FULL)):
                    t = pe.transpose(dst[:, P * (j - j0):P * (j - j0 + 1)], ctx_raw[:, j, :], ident[:, :])
                if c == NC - 1:
                    t = pe.transpose(dst[:, P * (FULL - j0):P * (FULL - j0) + TAIL],
                                     ctx_raw[0:TAIL, FULL, :], ident[0:TAIL, 0:TAIL])
                return t

            pe.wait_ge(ctx_loaded, 64)
            pe.wait_ge(xT_copied, 2)
            turn_ctx(ps_t[:, 0], 0).then_inc(ctx_turned, 1)
            turn_ctx(ps_t[:, 1], 1).then_inc(ctx_turned, 1)
            pe.wait_ge(xn_lo_done, 2)
            turn_ctx(ps_o[:, 0], 2).then_inc(ctx_turned, 1)

            for i in range(4):
                pe.wait_ge(wqk_lo_done, 4)
                for j in range(4):
                    h = 4 * i + j
                    w = head_cols(h)
                    t = three_pass(ps_s[:, i, Q * j:Q * (j + 1)], wqk_hi[:, w], wqk_lo[:, w],
                                   xn_hi[:, 0:Q], xn_lo[:, 0:Q])
                t.then_inc(q0_made, 1)
            pe.wait_ge(q0_lo_done, 4)

            def turn_wv(i):
                for j in range(4):
                    g = 4 * i + j
                    t = pe.transpose(WVT_BANKS[i][:, P * j:P * (j + 1)], wv_sb[:, P * g:P * (g + 1)], ident[:, :])
                t.then_inc(wvT_turned, 1)

            def make_wvo(i, bank):
                for j in range(4):
                    h = 2 * (4 * (i % 2) + j) + i // 2
                    at = slice(DH * (h % 2), DH * (h % 2) + DH)
                    t = pe.matmul(bank[:, P * j:P * (j + 1)], wvT[at, P * (h // 2):P * (h // 2) + P],
                                  wo_sb[at, h // 2, :], start=True, stop=True)
                t.then_inc(wvo_made, 1)

            def window(pe, b, par, first, last, nxt):
                def scores(s, c):
                    if not item_exists(s, first, last):
                        return
                    item = ITEMS[s]
                    m = rows(item)
                    kind, k = item_event(b, s, NC, c)
                    before = score_before(s, c, first, last)
                    if before is not None:
                        k2, v2 = item_event(b, before[0], NC, before[1])
                        pe.wait_ge(exped[k2], v2)
                    if c == 0 and item == LATE:
                        pe.wait_ge(x1_split, n(b - 1, 1, 0))
                    elif c == 0:
                        if s == 0:
                            pe.wait_ge(ctxT_lo, n(b, NC, NC - 1))
                        if not first:
                            pair = min(HP, -(-(TM * item + m) // (2 * Q)))
                            pe.wait_ge(q_lo_done, n(b - 1, HP, pair - 1))
                    c0, w = CHUNKS[c]
                    cp = 1 - par if item == LATE else par
                    if item == LATE:
                        a_hi, a_lo = x1_hi[:, :], x1_lo[:, :]
                    else:
                        a_hi, a_lo = q_hi[:, TM * item:TM * item + m], q_lo[:, TM * item:TM * item + m]
                    three_pass(ps_s[0:m, score_bank(s, c, par), 0:w], a_hi, a_lo,
                               cT_hi[cp][:, c0:c0 + w], cT_lo[cp][:, c0:c0 + w]).then_inc(scored[kind], 1)

                def wait_bank(what, s, c):
                    before = turn_before(b, what, s, c, first, last, nxt)
                    if before is not None:
                        pe.wait_ge(*before)

                def turn(s, c):
                    if not ((s < 0 and not first) or (s >= 0 and item_exists(s, first, last))):
                        return
                    m = rows(ITEMS[s])
                    kind, k = item_event(b, s, NC, c)
                    pe.wait_ge(exped[kind], k)
                    wait_bank("item", s, c)
                    bank = turn_bank("item", s, c, par)
                    j0, nj = TILE_SLOTS[c]
                    for j in range(j0, j0 + nj):
                        if j < FULL:
                            src = probs[s % 2][0:m, P * j:P * (j + 1)]
                        else:
                            kind2, k2 = item_event(b, s)
                            pe.wait_ge(tail_split[kind2], k2)
                            src = tails[s % 2][0:m, :]
                        t = pe.transpose(ps_t[:, bank, m * (j - j0):m * (j - j0 + 1)], src, ident[0:m, 0:m])
                    t.then_inc(turned[kind], 1)

                def passes(g, gb, cp):
                    w = Q if g == LATE else group_width(g)
                    col = LATE_COL if g == LATE else 0
                    buf = (NG * gb + (LATE_GROUP if g == LATE else g)) % 2
                    cols = slice(col, col + w)
                    whole, first_half = ps_o[:, 0, 0:2 * w].rearrange("p (a w) -> p a w", a=2), ps_o[:, 0, 0:w]
                    all_ = []
                    for j in range(FULL):
                        all_ += [(whole, c_hi[cp][:, j, :], pT_both[buf][:, j, :, cols]),
                                 (first_half, c_lo[cp][:, j, :], pT_both[buf][:, j, 0, cols])]
                    all_.append((first_half, c_hi[cp][:, FULL, :], pT_both[buf][:, FULL, 0, cols]))
                    return all_

                def pv(s, piece):
                    g, off, part, parts = PV_PLAN[s]
                    if (off < 0 and first) or (off >= 0 and last):
                        return
                    bb = b + off
                    par_b = (par + off) % 2
                    kind = "late" if g == LATE else "tile"
                    all_ = passes(g, par if g == LATE else par_b, par_b)
                    if part == 0 and piece == 0:
                        if g == LATE:
                            pe.wait_ge(turned_lo["late"], n(bb, NC, NC - 1))
                            pe.wait_ge(pv_out["tile"], n(b, NG, LATE_GROUP - 1) if not last else n(b - 1, NG, NG - 1))
                        else:
                            pe.wait_ge(turned_lo["tile"], n(bb, NT * NC, GROUPS[g][-1] * NC + NC - 1))
                            if g == LATE_GROUP and not first:
                                pe.wait_ge(pv_out["late"], n(b - 1, 1, 0))
                            else:
                                need(pe, pv_out["tile"], n(bb, NG, g) - 1)
                            if g == 0 and first:
                                pe.wait_ge(wvo_lo_done, 3)
                            if g == 0:
                                pe.wait_ge(ctx_lo_done, n(bb, len(CTX_SPLIT), len(CTX_SPLIT) - 1))
                                pe.wait_ge(stack_steps, n(bb, 3, 2))
                    at = part * PV_PIECES + piece
                    lo, hi = [len(all_) * (at + e) // (parts * PV_PIECES) for e in range(2)]
                    for i in range(lo, hi):
                        t = pe.matmul(*all_[i],
                                      start=(i == 0), stop=(i == len(all_) - 1))
                    if part == parts - 1 and piece == PV_PIECES - 1:
                        t.then_inc(pv_done[kind], 1)

                def misc(s):
                    if s in OUT_HEADS and not first:
                        heads = OUT_HEADS[s]
                        if heads[0] == 0:
                            if nxt:
                                pe.wait_ge(q_summed, n(b, HP, 0))
                            elif not last:
                                pe.wait_ge(q_summed, n(b - 1, HP, HP - 1))
                            if isinstance(b, int) or par == 1:
                                pe.wait_ge(wvo_lo_done, 4)
                        group = NG - 1 if heads[-1] == H - 1 else NG - 2
                        pe.wait_ge(o_split, n(b - 1, NG, group))
                        for h in heads:
                            w = head_cols(h)
                            t = three_pass_pair(ps_m[:, 0], 0, Q, wvo_hi[:, w], wvo_lo[:, w],
                                                o_both[:, :, Q * h:Q * (h + 1)],
                                                start=(h == 0), stop=(h == H - 1))
                        if heads[-1] == H - 1:
                            t.then_inc(proj_made, 1)
                    if s == ROW_STEP and not first:
                        pe.wait_ge(x1_ready, n(b - 1, 1, 0))
                        if nxt:
                            pe.wait_ge(q_summed, n(b, HP, 5))
                        pe.transpose(ps_m[0:Q, 0, 0:D], x1_T[:, :], ident[:, :]).then_inc(x1_turned, 1)
                    if s == FIN_STEP and not first:
                        pe.wait_ge(pv_out["late"], n(b - 1, 1, 0))
                        pe.wait_ge(x1_rows_ready, n(b - 1, 1, 0))
                        pe.transpose(ps_m[0:Q, 0, 0:D], late_T[:, :], ident[:, :]).then_inc(fin_turned, 1)
                    if pair_exists(s, first, last, nxt):
                        j, off = pair_at(s)
                        if first and j == 0:
                            pe.wait_ge(wvT_copied, 2)
                        elif first and j == 1:
                            pe.wait_ge(wvo_lo_done, 4)
                        elif first and j == 6:
                            pe.wait_ge(q_summed, n(b, HP, 5))
                        elif j == 1:
                            pe.wait_ge(x1_ready, n(b - 1, 1, 0))
                        elif j == 6:
                            pe.wait_ge(fin_ready, n(b - 1, 1, 0))
                        else:
                            need(pe, q_summed, n(b + off, HP, j) - 1)
                        xp = 1 - par if off == 0 else par
                        if j == 0:
                            pe.wait_ge(xb_ready, n(b, 2, 1))
                        for i in range(2):
                            w = head_cols(2 * j + i)
                            t = three_pass_pair(ps_m[:, 0], 2 * Q * i, Q, wqk_hi[:, w], wqk_lo[:, w],
                                                xb_both[xp][:, :, :])
                        t.then_inc(q_made, 1)
                    if first and s == 0:
                        pe.wait_ge(wvo_loaded, 32)
                        pe.wait_ge(ctxT_lo, 3)
                        turn_wv(0)
                        pe.wait_ge(xn_lo_done, 2)
                        turn_wv(1)
                    if first and s in WVO_PLAN:
                        for i, bank in WVO_PLAN[s]:
                            if i == 0:
                                pe.wait_ge(wvT_copied, 2)
                            elif i == 1:
                                pe.wait_ge(q_summed, 1)
                            else:
                                pe.wait_ge(wvo_lo_done, i - 1)
                            make_wvo(i, bank)

                for s in range(STEPS):
                    scores(s, 0)
                    turn(s - 1, 0)
                    scores(s, 1)
                    turn(s - 1, 1)
                    scores(s, 2)
                    pv(s, 0)
                    turn(s - 1, 2)
                    misc(s)
                    pv(s, 1)
                    if s in CTX_T_STEPS and nxt:
                        c = CTX_T_STEPS.index(s)
                        if c == 0:
                            pe.wait_ge(ctx_loaded, n(b + 1, 1, 0) * 64)
                        wait_bank("ctx", s, c)
                        turn_ctx(ps_t[:, turn_bank("ctx", s, c, par)], c).then_inc(ctx_turned, 1)

            windows(pe, window)


_INS = ['x', 'ctx_1024', 'L0_xattn_wq', 'L0_xattn_wk', 'L0_xattn_wv', 'L0_xattn_wo', 'L0_xattn_norm_w']
_OUTS = [((8, 100, 128), 'float32')]


def kernel(**inputs):
    import numpy as _np
    import concourse.bacc as _bacc
    from concourse import mybir as _mybir
    from concourse.bass_utils import run_bass_kernel_spmd as _run

    nc = _bacc.Bacc("TRN2", target_bir_lowering=False, num_devices=1)
    arrays, args = {}, []
    for name in _INS:
        a = _np.ascontiguousarray(inputs[name])
        arrays[f"in_{name}_dram"] = a
        args.append(nc.dram_tensor(f"in_{name}_dram", a.shape, _mybir.dt.from_np(a.dtype), kind="ExternalInput").ap())
    for i, (shape, dtype) in enumerate(_OUTS):
        dt = _mybir.dt.from_np(_np.dtype(dtype))
        args.append(nc.dram_tensor(f"out_{i}_dram", shape, dt, kind="ExternalOutput").ap())
    bass_two_cross_attentions(nc, *args)
    r = _run(nc, [arrays], core_ids=[0])
    return r.results[0]["out_0_dram"]
```

```python
from contextlib import ExitStack

import concourse.bass as bass
from concourse import mybir

F32 = mybir.dt.float32
F32R = mybir.dt.float32r
ALU = mybir.AluOpType
ACT = mybir.ActivationFunctionType
AX = mybir.AxisListType

EPS = 1e-6
DH = 64
P = 128


def bass_two_cross_attentions(nc, x, ctx_in, wq, wk, wv, wo, norm_w, out):
    B, Q, D = x.shape
    S = ctx_in.shape[1]
    H = wq.shape[1] // DH
    HP = H // 2
    R = H * Q
    TM = 124
    NT = -(-R // TM)
    FULL = S // P
    TAIL = S - FULL * P
    SLOTS = FULL + 1
    assert D == P and 3 * TAIL <= P and R % 2 == 0 and B % 2 == 0

    LATE = -1
    ITEMS = [0, 1, 2, 3, 4, 5, 6, 7, LATE, 8, 9, 10, 11, 12]
    STEPS = len(ITEMS)
    LATE_AT = ITEMS.index(LATE)
    CHUNKS = [(0, 512), (512, 512), (1024, S - 1024)]
    NC = len(CHUNKS)
    TILE_SLOTS = [(0, 4), (4, 4), (8, 4)]
    GROUPS = [(0, 1), (2, 3), (4, 5), (6, 7), (8,), (9, 10), (11, 12)]
    NG = len(GROUPS)
    LATE_GROUP, LATE_COL = 4, TM
    GW = 2 * TM

    def rows(item):
        return Q if item == LATE else min(TM, R - TM * item)

    def group_of(item):
        return LATE_GROUP if item == LATE else [g for g in range(NG) if item in GROUPS[g]][0]

    def group_col(item):
        return LATE_COL if item == LATE else TM * GROUPS[group_of(item)].index(item)

    def group_width(g):
        return sum(rows(t) for t in GROUPS[g])

    PV_PLAN = {0: (5, -1, 1, 2), 1: (6, -1, 0, 2), 2: (6, -1, 1, 2),
               3: (0, 0, 0, 2), 4: (0, 0, 1, 2), 5: (1, 0, 0, 2), 6: (1, 0, 1, 2),
               7: (2, 0, 0, 2), 8: (2, 0, 1, 2), 9: (3, 0, 0, 2), 10: (3, 0, 1, 2),
               11: (LATE, -1, 0, 1), 12: (4, 0, 0, 1), 13: (5, 0, 0, 2)}
    PV_CUTS = {1: (0, 11, 23), 2: (0, 4, 10, 14, 23)}
    assert all(cuts[-1] == 2 * FULL + 1 for cuts in PV_CUTS.values())
    PV_LAST = {(g, off): s for s, (g, off, part, parts) in PV_PLAN.items() if part == parts - 1}
    PAIR_STEPS = {1: 0, 6: 1, 7: 2, 8: 3, 9: 4, 10: 5, 13: 6}
    LAST_PAIR_STEP = 0
    FIRST_PAIR_STEPS = {0: 1, 1: 2, 2: 3, 3: 4, 4: 5, 5: 6, 6: 7}
    OUT_HEADS = {2: range(0, 5), 3: range(5, 9), 4: range(9, 13), 5: range(13, 16)}
    LAST_OUT_HEADS = {0: range(0, 9), 4: range(9, 13), 5: range(13, 16)}
    OUT_STEP = max(OUT_HEADS)
    ROW_STEP = 11
    FIN_STEP = 12
    CTX_T_STEPS = [9, 10, 11]
    CTX_SPLIT = [(0, 4), (4, 8), (8, 12)]
    CTX_SPLIT_STEPS = {12: (0, 1), 13: (1, 1), 0: (2, 0)}
    STACK_STEP = 1

    def n(b, per_batch, index):
        return b * per_batch + index + 1

    def need(eng, sem, value):
        if not (isinstance(value, int) and value <= 0):
            eng.wait_ge(sem, value)

    def head_cols(h):
        at = (h % 2) * HP + h // 2
        return slice(P * at, P * (at + 1))

    scratch = nc.dram_tensor("denominator_rows", [B, NT * TM], F32).ap()

    with ExitStack() as stack:
        def sb(name, shape, dt=F32):
            return stack.enter_context(nc.sbuf_tensor(name, shape, dt))

        def sem(name):
            return stack.enter_context(nc.semaphore(name))

        ident = sb("ident", [P, P])
        lo_rows = sb("lo_rows", [P, 1])
        hi_rows = sb("hi_rows", [P, 1])
        norm_col = sb("norm_col", [P, 1])
        x_T = sb("x_T", [P, B * Q])
        xn_T = sb("xn_T", [P, B * Q])
        wqk = sb("wqk", [P, H * D])
        wvo = sb("wvo", [P, H * D])
        q_hi = sb("q_hi", [P, 2, R], F32R)
        q_lo = sb("q_lo", [P, 2, R], F32R)
        ctx_raw = sb("ctx_raw", [P, SLOTS, D])
        c_hi = [sb(f"c_hi{i}", [P, SLOTS, D], F32R) for i in range(2)]
        c_lo = [sb(f"c_lo{i}", [P, FULL, D], F32R) for i in range(2)]
        cT_hi = [sb(f"cT_hi{i}", [P, S], F32R) for i in range(2)]
        cT_lo = [sb(f"cT_lo{i}", [P, S], F32R) for i in range(2)]
        tail_a = sb("tail_a", [P, D])
        tail_b = sb("tail_b", [P, D])
        probs = [sb(f"probs{i}", [P, S]) for i in range(2)]
        tails = [sb(f"tails{i}", [P, P]) for i in range(2)]
        part_max = sb("part_max", [P, STEPS, NC])
        neg_max = sb("neg_max", [P, STEPS])
        sums = sb("sums", [P, STEPS, NC])
        denom = sb("denom", [P, STEPS])
        rinv = sb("rinv", [P, STEPS])
        rinv_row = sb("rinv_row", [P, 2, GW])
        o_part = sb("o_part", [P, GW])
        o_raw = sb("o_raw", [P, GW])
        o_norm = sb("o_norm", [P, R])
        x1_T = sb("x1_T", [P, Q])
        x1_hi = sb("x1_hi", [P, Q], F32R)
        x1_lo = sb("x1_lo", [P, Q], F32R)
        x1_rows = sb("x1_rows", [P, D])
        late_T = sb("late_T", [P, Q])
        result = sb("result", [P, D])
        stats = sb("stats", [P, 7, B])
        wv_sb = sb("wv_sb", [P, H * DH])
        wo_sb = sb("wo_sb", [P, HP, D])
        wvT = sb("wvT", [P, HP * D])
        xb = sb("xb", [P, 2 * Q])

        def staging(names):
            with ExitStack() as early:
                return [early.enter_context(nc.sbuf_tensor(name, shape, F32)) for name, shape in names]

        wq_sb, wk_sb, x_sq = staging([("wq_sb", [P, H * DH]), ("wk_sb", [P, H * DH]), ("x_sq", [P, B, D])])
        pT_both = [sb("pT_both0", [P, SLOTS, 2, GW], F32R)]
        wqT, wkT, x_rows, xn_rows = staging([("wqT", [P, HP * D]), ("wkT", [P, HP * D]),
                                             ("x_rows", [P, B, D]), ("xn_rows", [P, B, D])])
        pT_both.append(sb("pT_both1", [P, SLOTS, 2, GW], F32R))

        def ps(name, banks):
            return stack.enter_context(nc.psum_tensor(name, [P, banks, 512], F32))

        ps_s = ps("ps_s", 4)
        ps_t = ps("ps_t", 2)
        ps_o = ps("ps_o", 1)
        ps_m = ps("ps_m", 1)

        WQK_BANKS = [(0, ps_s[:, 0]), (2, ps_s[:, 2]), (1, ps_o[:, 0]), (3, ps_t[:, 0])]
        PAIR0_BANK = ps_s[:, 0]
        CTX0_BANKS = [ps_t[:, 0], ps_t[:, 1], ps_s[:, 3]]
        CTX0_SPLIT_STEPS = {0: (0, 1), 1: (2,)}
        WVT_STEPS = {7: 0, 8: 1}
        WVO_STEPS = {9: 0, 10: 1, 11: 2, 12: 3}

        x_loaded = sem("x_loaded")
        wq_loaded = [sem(f"wq_loaded{i}") for i in range(2)]
        wk_loaded = [sem(f"wk_loaded{i}") for i in range(2)]
        wvo_loaded = sem("wvo_loaded")
        norm_loaded = sem("norm_loaded")
        ctx_loaded = sem("ctx_loaded")
        consts_begun = sem("consts_begun")
        consts_ready = sem("consts_ready")
        ident_begun = sem("ident_begun")
        ident_ready = sem("ident_ready")
        x_squared = sem("x_squared")
        x_meansq = sem("x_meansq")
        x_root = sem("x_root")
        x_newton = sem("x_newton")
        xn_ready = sem("xn_ready")
        wT_turned = sem("wT_turned")
        wqT_copied = sem("wqT_copied")
        wkT_copied = sem("wkT_copied")
        wqk_made = sem("wqk_made")
        wqk_ready = sem("wqk_ready")
        xn_turned = sem("xn_turned")
        x_turned = sem("x_turned")
        xT_copied = sem("xT_copied")
        xnT_copied = sem("xnT_copied")
        wvT_turned = sem("wvT_turned")
        wvT_copied = sem("wvT_copied")
        wvo_made = sem("wvo_made")
        wvo_ready = sem("wvo_ready")
        kinds = ("tile", "late")
        scored = {k: sem(f"scored_{k}") for k in kinds}
        chunk_max = {k: sem(f"chunk_max_{k}") for k in kinds}
        maxed = {k: sem(f"maxed_{k}") for k in kinds}
        exped = {k: sem(f"exped_{k}") for k in kinds}
        tail_hi = {k: sem(f"tail_hi_{k}") for k in kinds}
        tail_split = {k: sem(f"tail_split_{k}") for k in kinds}
        turned = {k: sem(f"turned_{k}") for k in kinds}
        turned_hi = {k: sem(f"turned_hi_{k}") for k in kinds}
        turned_lo = {k: sem(f"turned_lo_{k}") for k in kinds}
        denom_sum = {k: sem(f"denom_sum_{k}") for k in kinds}
        inverted = {k: sem(f"inverted_{k}") for k in kinds}
        pv_done = {k: sem(f"pv_done_{k}") for k in kinds}
        pv_part_out = {k: sem(f"pv_part_out_{k}") for k in kinds}
        pv_out = {k: sem(f"pv_out_{k}") for k in kinds}
        ctx_turned = sem("ctx_turned")
        ctxT_hi = sem("ctxT_hi")
        ctxT_lo = sem("ctxT_lo")
        ctx_hi_done = sem("ctx_hi_done")
        ctx_lo_done = sem("ctx_lo_done")
        stack_steps = sem("stack_steps")
        tail_masked = sem("tail_masked")
        rinv_stored = sem("rinv_stored")
        rinv_row_loaded = [sem(f"rinv_row_loaded{g}") for g in range(NG)]
        o_normed = sem("o_normed")
        xb_ready = sem("xb_ready")
        q_made = sem("q_made")
        q_hi_done = sem("q_hi_done")
        q_lo_done = sem("q_lo_done")
        proj_made = sem("proj_made")
        x1_ready = sem("x1_ready")
        x1_hi_done = sem("x1_hi_done")
        x1_split = sem("x1_split")
        x1_turned = sem("x1_turned")
        x1_rows_ready = sem("x1_rows_ready")
        fin_turned = sem("fin_turned")
        fin_ready = sem("fin_ready")
        stored = sem("stored")
        pool_passed = sem("pool_passed")
        sp_passed = sem("sp_passed")

        def item_exists(step, first, last):
            return not first if ITEMS[step] == LATE else not last

        def item_event(b, step, per_item=1, index=0):
            if step < 0:
                b, step = b - 1, step + STEPS
            if ITEMS[step] == LATE:
                return "late", n(b - 1, per_item, index)
            return "tile", n(b, NT * per_item, ITEMS[step] * per_item + index)

        def score_bank(step, c, par):
            return (NC * (STEPS * par + step) + c) % 4

        def score_before(step, c, first, last):
            at = NC * step + c
            while True:
                at -= 4
                s, k = at // NC, at % NC
                if s < 0:
                    return None if first else (s, k)
                if item_exists(s, first, last):
                    return s, k

        def probs_before(step, first, last):
            step -= 2
            while step >= 0 and not item_exists(step, first, last):
                step -= 2
            return None if step < 0 and first else step

        TURNS = []
        for s in range(STEPS):
            TURNS += [("item", s - 1, c) for c in range(NC)]
            if s in CTX_T_STEPS:
                TURNS.append(("ctx", s, CTX_T_STEPS.index(s)))

        def turn_exists(at, first, last, nxt):
            what, s, _ = TURNS[at]
            if what == "ctx":
                return nxt
            if s < 0:
                return not first
            return item_exists(s, first, last)

        def turn_bank(what, s, c, par):
            return (len(TURNS) * par + TURNS.index((what, s, c))) % 2

        def turn_before(b, what, s, c, first, last, nxt):
            at = TURNS.index((what, s, c))
            while True:
                at -= 2
                if at < 0:
                    if first:
                        return None
                    _, s2, c2 = TURNS[at % len(TURNS)]
                    k, v = item_event(b - 1, s2, NC, c2)
                    return turned_lo[k], v
                if turn_exists(at, first, last, nxt):
                    what2, s2, c2 = TURNS[at]
                    if what2 == "ctx":
                        return ctxT_lo, n(b + 1, NC, c2)
                    k, v = item_event(b, s2, NC, c2)
                    return turned_lo[k], v

        def group_buffer(item, par):
            return (NG * par + group_of(item)) % 2

        def pv_before_group(b, item):
            return n(b, NG, group_of(item) - 2)

        def groups_finished(s, first, last):
            for (g, off), at in PV_LAST.items():
                if (at + 1) % STEPS == s:
                    off -= at + 1 == STEPS
                    if not (first if off < 0 else last):
                        yield g, off

        def pair_at(s, par, first, last, nxt):
            if first:
                return (FIRST_PAIR_STEPS[s], 0) if s in FIRST_PAIR_STEPS else None
            if par == 1:
                return (PAIR_STEPS[s], 1) if nxt and s in PAIR_STEPS else None
            return (HP - 1, 0) if s == LAST_PAIR_STEP and not last else None

        def pairs_up_to(even, j):
            return even * (HP // 2) + j + 1

        def of_pair(q, j):
            return q[:, :, 2 * Q * j:2 * Q * (j + 1)].rearrange("p a (h q) -> p h a q", h=2)

        def in_bank(bank):
            return bank[:, 0:4 * Q].rearrange("p (h a q) -> p h a q", h=2, a=2)

        def windows(eng, body):
            body(eng, 0, 0, True, False, True)
            with eng.Fori(0, (B - 2) // 2) as i:
                body(eng, i * 2 + 1, 1, False, False, True)
                body(eng, i * 2 + 2, 0, False, False, True)
            body(eng, B - 1, 1, False, False, False)
            body(eng, B, 0, False, True, False)

        block = stack.enter_context(nc.Block())

        @block.sync
        def _(sp):
            def load_ctx(b):
                main = ctx_in[bass.ds(b, 1), 0:FULL * P, :].rearrange("a (p j) d -> p (a j) d", j=FULL)
                sp.dma_start(ctx_raw[:, 0:FULL, :], main).then_inc(ctx_loaded, 16)
                for k in range(3):
                    sp.dma_start(ctx_raw[k * TAIL:(k + 1) * TAIL, FULL, :],
                                 ctx_in[bass.ds(b, 1), FULL * P:S, :].rearrange("a t d -> (a t) d"))\
                        .then_inc(ctx_loaded, 16)

            sp.dma_start(x_rows[0:Q, :, :], x.rearrange("b q d -> q b d")).then_inc(x_loaded, 16)
            for i in range(2):
                half = slice(512 * i, 512 * (i + 1))
                sp.dma_start(wq_sb[:, half], wq[:, half]).then_inc(wq_loaded[i], 16)
                sp.dma_start(wk_sb[:, half], wk[:, half]).then_inc(wk_loaded[i], 16)
                if i == 0:
                    sp.dma_start(norm_col[:, :], norm_w.rearrange("(d a) -> d a", a=1)).then_inc(norm_loaded, 16)
                    sp.wait_ge(consts_begun, 1)
                    load_ctx(0)
            sp.dma_start(wv_sb[:, :], wv).then_inc(wvo_loaded, 16)
            sp.dma_start(wo_sb[:, :, :], wo.rearrange("(g e) d -> e g d", e=P)).then_inc(wvo_loaded, 16)

            def carry():
                sp.sem_inc(sp_passed, 1)

            def window(sp, b, par, first, last, nxt):
                if nxt:
                    sp.wait_ge(ctx_turned, n(b, NC, NC - 1))
                    sp.wait_ge(ctx_lo_done, n(b, len(CTX_SPLIT), len(CTX_SPLIT) - 1))
                    sp.wait_ge(stack_steps, n(b, 3, 2))
                    carry()
                    load_ctx(b + 1)
                for g in range(NG):
                    if not last:
                        t0, k = GROUPS[g][0], len(GROUPS[g])
                        s0 = ITEMS.index(t0)
                        cols = slice(TM * t0, TM * (t0 + k))
                        if g == NG - 1 and not first:
                            sp.wait_ge(stored, n(b - 1, 1, 0) * 16)
                            carry()
                        sp.wait_ge(inverted["tile"], n(b, NG, g))
                        carry()
                        sp.dma_start(scratch[bass.ds(b, 1), cols].rearrange("a (t p) -> p (a t)", p=TM),
                                     rinv[0:TM, s0:s0 + k],
                                     allow_slow_non_contiguous=True).then_inc(rinv_stored, 16)
                        sp.wait_ge(rinv_stored, n(b, NG, g) * 16)
                        carry()
                        need(sp, o_normed, n(b, NG, g - 2))
                        carry()
                        row = scratch[bass.ds(b, 1), cols]
                        sp.dma_start(rinv_row[:, (NG * par + g) % 2, 0:TM * k], row.to_broadcast([P, TM * k]))\
                            .then_inc(rinv_row_loaded[g], 16)
                    if g == NG - 2 and not first:
                        sp.wait_ge(fin_ready, n(b - 1, 1, 0))
                        carry()
                        sp.dma_start(out[bass.ds(b - 1, 1), :, :].rearrange("a q d -> (a q) d"),
                                     result[0:Q, :]).then_inc(stored, 16)

            windows(sp, window)
            sp.wait_ge(stored, 16 * B)

        @block.gpsimd
        def _(pool):
            pool.memset(ident[:, :], 0.0).then_inc(ident_begun, 1)
            pool.wait_ge(ident_begun, 1)
            pool.affine_select(out=ident[:, :], in_=ident[:, :], compare_op=ALU.not_equal, fill=1.0,
                               base=0, pattern=[[-1, P]], channel_multiplier=1).then_inc(ident_ready, 1)
            pool.memset(ctx_raw[:, FULL, :], 0.0).then_inc(consts_begun, 1)
            pool.memset(lo_rows[:, :], 1.0).then_inc(consts_begun, 1)
            for i in range(2):
                pool.memset(tails[i][:, :], 0.0).then_inc(consts_begun, 1)
            pool.memset(sums[:, :, :], 1.0).then_inc(consts_begun, 1)
            pool.wait_ge(consts_begun, 5)
            pool.affine_select(out=lo_rows[:, :], in_=lo_rows[:, :], compare_op=ALU.is_ge, fill=0.0,
                               base=-TAIL, pattern=[[0, 1]], channel_multiplier=1).then_inc(consts_ready, 1)
            pool.wait_ge(consts_ready, 1)
            pool.affine_select(out=lo_rows[:, :], in_=lo_rows[:, :], compare_op=ALU.is_ge, fill=0.0,
                               base=2 * TAIL - 1, pattern=[[0, 1]], channel_multiplier=-1).then_inc(consts_ready, 1)
            pool.wait_ge(consts_ready, 2)
            pool.tensor_scalar(hi_rows[:, :], lo_rows[:, :], -1.0, 1.0, ALU.mult, ALU.add)\
                .then_inc(consts_ready, 1)
            pool.wait_ge(consts_ready, 3)

            def carry():
                pool.sem_inc(pool_passed, 1)

            def split_ctx(b, par, part):
                lo, hi = CTX_SPLIT[part]
                top = min(hi, FULL)
                parts = len(CTX_SPLIT)
                src = ctx_raw[:, lo:top, :]
                pool.wait_ge(ctx_hi_done, n(b, parts, part))
                pool.tensor_tensor(c_lo[par][:, lo:top, :], src, c_hi[par][:, lo:top, :].bitcast(F32),
                                   ALU.subtract).then_inc(ctx_lo_done, 1)

            def stack_tail(b, par):
                raw = ctx_raw[:, FULL, :]
                carry()
                pool.tensor_copy(tail_a[:, :].bitcast(F32R), raw).then_inc(stack_steps, 1)
                pool.wait_ge(stack_steps, n(b, 3, 0))
                pool.tensor_tensor(tail_b[:, :], raw, tail_a[:, :], ALU.subtract).then_inc(stack_steps, 1)
                pool.wait_ge(stack_steps, n(b, 3, 1))
                carry()
                pool.tensor_scalar(tail_a[:, :], tail_a[:, :], hi_rows[:, 0:1], None, ALU.mult)\
                    .then_inc(tail_masked, 1)
                pool.tensor_scalar(tail_b[:, :], tail_b[:, :], lo_rows[:, 0:1], None, ALU.mult)\
                    .then_inc(tail_masked, 1)
                pool.wait_ge(tail_masked, n(b, 2, 1))
                pool.tensor_tensor(c_hi[par][:, FULL, :], tail_a[:, :], tail_b[:, :], ALU.add)\
                    .then_inc(stack_steps, 1)

            pool.wait_ge(ctx_loaded, 16 * 4)
            stack_tail(0, 0)
            pool.wait_ge(xnT_copied, 2)

            def window(pool, b, par, first, last, nxt):
                for s in range(STEPS):
                    if s == 0 and par == 1 and nxt:
                        pool.wait_ge(q_made, pairs_up_to(b - 1, HP - 1))
                        carry()
                        pool.tensor_copy(xb[:, :], xn_T[:, bass.ds((b + 1) * Q, 2 * Q)])\
                            .then_inc(xb_ready, 2)
                    for g, off2 in groups_finished(s, first, last):
                        if g == LATE or (last and g == NG - 1):
                            continue
                        bb = b + off2
                        w = group_width(g)
                        cols = slice(TM * GROUPS[g][0], TM * GROUPS[g][0] + w)
                        pool.wait_ge(rinv_row_loaded[g], n(bb, 1, 0) * 16)
                        pool.wait_ge(pv_out["tile"], n(bb, NG, g))
                        if g == 0:
                            need(pool, proj_made, n(bb - 1, 1, 0))
                        pool.tensor_tensor(o_norm[:, cols], o_raw[:, 0:w],
                                           rinv_row[:, (NG * ((par + off2) % 2) + g) % 2, 0:w], ALU.mult)\
                            .then_inc(o_normed, 1)
                    if item_exists(s, first, last):
                        item = ITEMS[s]
                        m = rows(item)
                        kind, k = item_event(b, s, NC, NC - 1)
                        pool.wait_ge(exped[kind], k)
                        before = probs_before(s, first, last)
                        if before is not None:
                            kind2, k2 = item_event(b, before, NC, NC - 1)
                            pool.wait_ge(turned[kind2], k2)
                        t = tails[s % 2]
                        src = probs[s % 2][0:m, FULL * P:S]
                        carry()
                        for c in range(2):
                            pool.tensor_copy(t[0:m, c * TAIL:(c + 1) * TAIL].bitcast(F32R), src)\
                                .then_inc(tail_hi[kind], 1)
                        _, k = item_event(b, s, 2, 1)
                        pool.wait_ge(tail_hi[kind], k)
                        pool.tensor_tensor(t[0:m, 2 * TAIL:3 * TAIL].bitcast(F32R), src, t[0:m, 0:TAIL],
                                           ALU.subtract).then_inc(tail_split[kind], 1)
                    if s == OUT_STEP and not first and not last:
                        pool.wait_ge(x1_ready, n(b - 1, 1, 0))
                        carry()
                        pool.tensor_copy(x1_hi[:, :], x1_T[:, :]).then_inc(x1_hi_done, 1)
                        pool.wait_ge(x1_hi_done, n(b - 1, 1, 0))
                        pool.tensor_tensor(x1_lo[:, :], x1_T[:, :], x1_hi[:, :].bitcast(F32),
                                           ALU.subtract).then_inc(x1_split, 1)
                    if s in CTX_SPLIT_STEPS:
                        part, off = CTX_SPLIT_STEPS[s]
                        if nxt if off else not (first or last):
                            split_ctx(b + off, (par + off) % 2, part)
                    if first and s in CTX0_SPLIT_STEPS:
                        for part in CTX0_SPLIT_STEPS[s]:
                            split_ctx(0, 0, part)
                    if s == STACK_STEP and not (first or last):
                        stack_tail(b, par)

            windows(pool, window)

        @block.scalar
        def _(act):
            def copy_wqT(half):
                act.wait_ge(wT_turned, 2 * half + 1)
                act.activation(wqT[:, 512 * half:512 * (half + 1)], ps_t[:, 0, :], ACT.Copy).then_inc(wqT_copied, 1)

            def copy_wkT(half):
                act.wait_ge(wT_turned, 2 * half + 2)
                act.activation(wkT[:, 512 * half:512 * (half + 1)], ps_t[:, 1, :], ACT.Copy).then_inc(wkT_copied, 1)

            def copy_wqk(k):
                i, bank = WQK_BANKS[k]
                act.wait_ge(wqk_made, k + 1)
                act.activation(wqk[:, 512 * i:512 * (i + 1)], bank, ACT.Copy,
                               scale=norm_col[:, 0:1]).then_inc(wqk_ready, 1)

            def pair_hi(even, j, bank):
                act.wait_ge(q_made, pairs_up_to(even, j))
                act.activation(of_pair(q_hi, j), in_bank(bank), ACT.Copy).then_inc(q_hi_done, 1)

            act.wait_ge(consts_begun, 3)
            act.activation(stats[0:Q, 6, :], tails[0][0:Q, 0:B], ACT.Sqrt)
            copy_wqT(0)
            act.wait_ge(x_meansq, 2)
            act.activation(stats[0:Q, 2, :], stats[0:Q, 1, :], ACT.Sqrt).then_inc(x_root, 1)
            copy_wkT(0)
            act.wait_ge(x_root, 1)
            act.activation(stats[0:Q, 6, :], stats[0:Q, 2, :], ACT.Exp)
            act.wait_ge(norm_loaded, 16)
            for i in range(2):
                copy_wqk(i)
                act.wait_ge(xn_turned, i + 1)
                act.activation(xn_T[:, 400 * i:400 * (i + 1)], (ps_o, ps_m)[i][:, 0, 0:400], ACT.Copy)\
                    .then_inc(xnT_copied, 1)
            for c, (c0, w) in enumerate(CHUNKS):
                act.wait_ge(ctx_turned, c + 1)
                act.activation(cT_hi[0][:, c0:c0 + w], CTX0_BANKS[c][:, 0:w], ACT.Copy).then_inc(ctxT_hi, 1)
            pair_hi(0, 0, PAIR0_BANK)
            for i in range(2):
                act.wait_ge(x_turned, i + 1)
                act.activation(x_T[:, 400 * i:400 * (i + 1)], (ps_o, ps_m)[i][:, 0, 0:400], ACT.Copy)\
                    .then_inc(xT_copied, 1)

            def ctx_hi(b, par, part):
                lo, hi = CTX_SPLIT[part]
                top = min(hi, FULL)
                act.activation(c_hi[par][:, lo:top, :], ctx_raw[:, lo:top, :], ACT.Copy).then_inc(ctx_hi_done, 1)

            act.wait_ge(consts_ready, 3)

            def window(act, b, par, first, last, nxt):
                def split_ctx_hi(s):
                    if s not in CTX_SPLIT_STEPS:
                        return
                    part, off = CTX_SPLIT_STEPS[s]
                    if nxt if off else not (first or last):
                        if part == 0:
                            act.wait_ge(ctx_loaded, n(b + 1, 1, 0) * 64)
                            if not first:
                                act.wait_ge(pv_done["late"], n(b - 1, 1, 0))
                        ctx_hi(b + off, (par + off) % 2, part)

                def turned_ctx_hi(s):
                    if not (s in CTX_T_STEPS and nxt):
                        return
                    c = CTX_T_STEPS.index(s)
                    c0, w = CHUNKS[c]
                    act.wait_ge(ctx_turned, n(b + 1, NC, c))
                    if c == 0 and not first:
                        act.wait_ge(scored["late"], n(b - 1, NC, NC - 1))
                    act.activation(cT_hi[1 - par][:, c0:c0 + w],
                                   ps_t[:, turn_bank("ctx", s, c, par), 0:w], ACT.Copy).then_inc(ctxT_hi, 1)

                for s in range(STEPS):
                    for g, off2 in groups_finished(s, first, last):
                        kind = "late" if g == LATE else "tile"
                        w = Q if g == LATE else group_width(g)
                        act.wait_ge(pv_done[kind], n(b - 1, 1, 0) if g == LATE else n(b + off2, NG, g))
                        act.activation(o_part[:, 0:w], ps_o[:, 0, w:2 * w], ACT.Copy)\
                            .then_inc(pv_part_out[kind], 1)
                    if last and s == OUT_STEP:
                        act.wait_ge(x1_ready, n(b - 1, 1, 0))
                        act.activation(x1_hi[:, :], x1_T[:, :], ACT.Copy).then_inc(x1_hi_done, 1)
                    prev = s - 1
                    if (prev < 0 and not first) or (prev >= 0 and item_exists(prev, first, last)):
                        item = ITEMS[prev]
                        m, col = rows(item), group_col(item)
                        pb = 1 - par if prev < 0 else par
                        buf = group_buffer(item, pb)
                        bank_par = par
                        wb = b - 1 if prev < 0 else b
                        for c, (j0, nj) in enumerate(TILE_SLOTS):
                            kind, k = item_event(b, prev, NC, c)
                            act.wait_ge(turned[kind], k)
                            if c == 0:
                                need(act, pv_done["tile"], n(wb - 1, NG, NG - 1) if last and item == LATE
                                     else pv_before_group(wb, item))
                                if group_of(item) == LATE_GROUP + 2:
                                    need(act, pv_done["late"], n(wb - 1, 1, 0))
                            bank = turn_bank("item", prev, c, bank_par)
                            act.activation(pT_both[buf][:, j0:j0 + nj, 0, col:col + m],
                                           ps_t[:, bank, 0:nj * m].rearrange("p (j m) -> p j m", m=m),
                                           ACT.Copy).then_inc(turned_hi[kind], 1)
                            if c == 1:
                                split_ctx_hi(s)
                    if first and s == 0:
                        copy_wqT(1)
                        copy_wkT(1)
                    pair = pair_at(s, par, first, last, nxt)
                    if pair is not None and not item_exists(s, first, last):
                        pair_hi(b + pair[1], pair[0], ps_m[:, 0])
                    if item_exists(s, first, last):
                        m = rows(ITEMS[s])
                        kind, k = item_event(b, s)
                        act.wait_ge(maxed[kind], k)
                        before = probs_before(s, first, last)
                        for c, (c0, w) in enumerate(CHUNKS):
                            if before is not None:
                                kind2, k2 = item_event(b, before, NC, c)
                                act.wait_ge(turned[kind2], k2)
                            act.activation(probs[s % 2][0:m, c0:c0 + w],
                                           ps_s[0:m, score_bank(s, c, par), 0:w], ACT.Exp,
                                           bias=neg_max[0:m, s:s + 1],
                                           accum_out=sums[0:m, s, c:c + 1]).then_inc(exped[kind], 1)
                            if c == 1 and pair is not None:
                                pair_hi(b + pair[1], pair[0], ps_m[:, 0])
                            if c == 1:
                                turned_ctx_hi(s)
                    if first and s == 0:
                        copy_wqk(2)
                        copy_wqk(3)
                    if first and s in CTX0_SPLIT_STEPS:
                        for part in CTX0_SPLIT_STEPS[s]:
                            ctx_hi(0, 0, part)
                    if first and s in WVT_STEPS:
                        i = WVT_STEPS[s]
                        act.wait_ge(wvT_turned, i + 1)
                        act.activation(wvT[:, 512 * i:512 * (i + 1)], ps_m[:, 0], ACT.Copy).then_inc(wvT_copied, 1)
                    if first and s in WVO_STEPS:
                        i = WVO_STEPS[s]
                        act.wait_ge(wvo_made, i + 1)
                        act.activation(wvo[:, 512 * i:512 * (i + 1)], ps_m[:, 0], ACT.Copy)\
                            .then_inc(wvo_ready, 1)

            windows(act, window)

        @block.vector
        def _(dve):
            dve.wait_ge(x_loaded, 16)
            dve.tensor_tensor(x_sq[0:Q, :, :], x_rows[0:Q, :, :], x_rows[0:Q, :, :], ALU.mult)\
                .then_inc(x_squared, 1)
            dve.wait_ge(x_squared, 1)
            dve.tensor_reduce(stats[0:Q, 0, :], x_sq[0:Q, :, :], AX.X, ALU.add).then_inc(x_meansq, 1)
            dve.wait_ge(x_meansq, 1)
            dve.tensor_scalar(stats[0:Q, 1, :], stats[0:Q, 0, :], 1.0 / D, EPS, ALU.mult, ALU.add)\
                .then_inc(x_meansq, 1)
            dve.wait_ge(x_root, 1)
            dve.reciprocal(stats[0:Q, 3, :], stats[0:Q, 2, :]).then_inc(x_newton, 1)
            dve.wait_ge(x_newton, 1)
            dve.tensor_tensor(stats[0:Q, 4, :], stats[0:Q, 3, :], stats[0:Q, 3, :], ALU.mult)\
                .then_inc(x_newton, 1)
            dve.wait_ge(x_newton, 2)
            dve.tensor_tensor(stats[0:Q, 5, :], stats[0:Q, 4, :], stats[0:Q, 1, :], ALU.mult)\
                .then_inc(x_newton, 1)
            dve.wait_ge(x_newton, 3)
            dve.tensor_scalar(stats[0:Q, 4, :], stats[0:Q, 5, :], -0.5, 1.5, ALU.mult, ALU.add)\
                .then_inc(x_newton, 1)
            dve.wait_ge(x_newton, 4)
            dve.tensor_tensor(stats[0:Q, 5, :], stats[0:Q, 4, :], stats[0:Q, 3, :], ALU.mult)\
                .then_inc(x_newton, 1)
            dve.wait_ge(x_newton, 5)
            for i in range(B):
                dve.tensor_scalar(xn_rows[0:Q, i, :], x_rows[0:Q, i, :], stats[0:Q, 5, i:i + 1], None,
                                  ALU.mult).then_inc(xn_ready, 1)
            def lo_part(dst, src, hi, done):
                dve.tensor_tensor(dst, src, hi.bitcast(F32), ALU.subtract).then_inc(done, 1)

            def pair_lo(even, j, bank):
                dve.wait_ge(q_hi_done, pairs_up_to(even, j))
                lo_part(of_pair(q_lo, j), in_bank(bank), of_pair(q_hi, j), q_lo_done)

            for c, (c0, w) in enumerate(CHUNKS):
                dve.wait_ge(ctxT_hi, c + 1)
                lo_part(cT_lo[0][:, c0:c0 + w], CTX0_BANKS[c][:, 0:w], cT_hi[0][:, c0:c0 + w], ctxT_lo)
            pair_lo(0, 0, PAIR0_BANK)

            def invert(b, steps, kind, per, index, m):
                k, v = item_event(b, steps[-1], NC, NC - 1)
                dve.wait_ge(exped[k], v)
                lo, hi = steps[0], steps[-1] + 1
                dve.tensor_reduce(denom[0:m, lo:hi], sums[0:m, lo:hi, :], AX.X, ALU.add)\
                    .then_inc(denom_sum[kind], 1)
                dve.wait_ge(denom_sum[kind], n(b, per, index))
                dve.reciprocal(rinv[0:m, lo:hi], denom[0:m, lo:hi]).then_inc(inverted[kind], 1)

            def window(dve, b, par, first, last, nxt):
                for s in range(STEPS):
                    for g, off2 in groups_finished(s, first, last):
                        if g == LATE:
                            dve.wait_ge(pv_part_out["late"], n(b - 1, 1, 0))
                            dve.tensor_tensor(late_T[:, :], ps_o[:, 0, 0:Q], o_part[:, 0:Q], ALU.add)\
                                .then_inc(pv_out["late"], 1)
                        else:
                            w = group_width(g)
                            dve.wait_ge(pv_part_out["tile"], n(b + off2, NG, g))
                            need(dve, o_normed, n(b + off2, NG, g) - 1)
                            dve.tensor_tensor(o_raw[:, 0:w], ps_o[:, 0, 0:w], o_part[:, 0:w], ALU.add)\
                                .then_inc(pv_out["tile"], 1)
                            if last and g == NG - 1:
                                cols = slice(TM * GROUPS[g][0], TM * GROUPS[g][0] + w)
                                dve.wait_ge(rinv_row_loaded[g], n(b - 1, 1, 0) * 16)
                                dve.wait_ge(pv_out["tile"], n(b - 1, NG, g))
                                dve.tensor_tensor(o_norm[:, cols], o_raw[:, 0:w],
                                                  rinv_row[:, (NG * ((par + off2) % 2) + g) % 2, 0:w], ALU.mult)\
                                    .then_inc(o_normed, 1)

                    here = item_exists(s, first, last)
                    prev = s - 1
                    there = (prev < 0 and not first) or (prev >= 0 and item_exists(prev, first, last))

                    def chunk_maximum(c):
                        if not here:
                            return
                        m = rows(ITEMS[s])
                        kind, k = item_event(b, s, NC, c)
                        dve.wait_ge(scored[kind], k)
                        mx = dve.tensor_reduce(part_max[0:m, s, c:c + 1],
                                               ps_s[0:m, score_bank(s, c, par), 0:CHUNKS[c][1]],
                                               AX.X, ALU.max)
                        if c == NC - 1:
                            mx.then_inc(chunk_max[kind], 1)
                            kind, k = item_event(b, s)
                            dve.wait_ge(chunk_max[kind], k)
                            dve.tensor_reduce(neg_max[0:m, s:s + 1], part_max[0:m, s, :], AX.X, ALU.max,
                                              negate=True).then_inc(maxed[kind], 1)

                    def turned_chunk_lo(c):
                        if not there:
                            return
                        item = ITEMS[prev]
                        m, col = rows(item), group_col(item)
                        buf = group_buffer(item, 1 - par if prev < 0 else par)
                        kind, k = item_event(b, prev, NC, c)
                        dve.wait_ge(turned_hi[kind], k)
                        j0, nj = TILE_SLOTS[c]
                        nj = min(nj, FULL - j0)
                        bank = turn_bank("item", prev, c, par)
                        lo_part(pT_both[buf][:, j0:j0 + nj, 1, col:col + m],
                                ps_t[:, bank, 0:nj * m].rearrange("p (j m) -> p j m", m=m),
                                pT_both[buf][:, j0:j0 + nj, 0, col:col + m], turned_lo[kind])

                    chunk_maximum(0)
                    turned_chunk_lo(0)
                    chunk_maximum(1)
                    chunk_maximum(2)
                    turned_chunk_lo(1)
                    turned_chunk_lo(2)

                    if s in CTX_T_STEPS and nxt:
                        c = CTX_T_STEPS.index(s)
                        c0, w = CHUNKS[c]
                        dve.wait_ge(ctxT_hi, n(b + 1, NC, c))
                        lo_part(cT_lo[1 - par][:, c0:c0 + w], ps_t[:, turn_bank("ctx", s, c, par), 0:w],
                                cT_hi[1 - par][:, c0:c0 + w], ctxT_lo)
                    if prev < 0:
                        if not first:
                            invert(b - 1, [12, 13], "tile", NG, NG - 1, TM)
                    elif there:
                        if ITEMS[prev] == LATE:
                            k, v = item_event(b, prev, NC, NC - 1)
                            dve.wait_ge(exped[k], v)
                            dve.tensor_reduce(denom[0:Q, prev:prev + 1], sums[0:Q, prev, :], AX.X, ALU.add)\
                                .then_inc(denom_sum["late"], 1)
                            dve.wait_ge(denom_sum["late"], n(b - 1, 1, 0))
                            dve.reciprocal(rinv[0:Q, prev:prev + 1], denom[0:Q, prev:prev + 1])\
                                .then_inc(inverted["late"], 1)
                        else:
                            g = group_of(ITEMS[prev])
                            if ITEMS[prev] == GROUPS[g][-1]:
                                invert(b, [ITEMS.index(t) for t in GROUPS[g]], "tile", NG, g, TM)
                    pair = pair_at(s, par, first, last, nxt)
                    if pair is not None:
                        pair_lo(b + pair[1], pair[0], ps_m[:, 0])
                    if s == OUT_STEP and not first:
                        dve.wait_ge(proj_made, n(b - 1, 1, 0))
                        dve.wait_ge(xT_copied, 2)
                        dve.tensor_tensor(x1_T[:, :], ps_m[:, 0, 0:Q], x_T[:, bass.ds((b - 1) * Q, Q)],
                                          ALU.add).then_inc(x1_ready, 1)
                        if last:
                            dve.wait_ge(x1_hi_done, n(b - 1, 1, 0))
                            lo_part(x1_lo[:, :], x1_T[:, :], x1_hi[:, :], x1_split)
                    if s == ROW_STEP and not first:
                        dve.wait_ge(x1_turned, n(b - 1, 1, 0))
                        if last:
                            dve.wait_ge(fin_ready, n(b - 2, 1, 0))
                        dve.tensor_copy(x1_rows[0:Q, :], ps_m[0:Q, 0, 0:D]).then_inc(x1_rows_ready, 1)
                    if s == FIN_STEP and not first:
                        dve.wait_ge(fin_turned, n(b - 1, 1, 0))
                        dve.wait_ge(inverted["late"], n(b - 1, 1, 0))
                        dve.wait_ge(x1_rows_ready, n(b - 1, 1, 0))
                        dve.scalar_tensor_tensor(out=result[0:Q, :], in0=ps_m[0:Q, 0, 0:D],
                                                 scalar=rinv[0:Q, LATE_AT:LATE_AT + 1],
                                                 in1=x1_rows[0:Q, :], op0=ALU.mult, op1=ALU.add)\
                            .then_inc(fin_ready, 1)

            windows(dve, window)

        @block.tensor
        def _(pe):
            pe.wait_ge(ident_ready, 1)

            def turn_weights(half):
                for i, (src, loaded) in enumerate(((wq_sb, wq_loaded), (wk_sb, wk_loaded))):
                    pe.wait_ge(loaded[half], 16)
                    if half == 1:
                        pe.wait_ge(ctxT_lo, i + 1)
                    for j in range(4):
                        g = 4 * half + j
                        t = pe.transpose(ps_t[:, i, P * j:P * (j + 1)], src[:, P * g:P * (g + 1)], ident[:, :])
                    t.then_inc(wT_turned, 1)

            def make_wqk(k):
                i, bank = WQK_BANKS[k]
                pe.wait_ge(wqT_copied, i % 2 + 1)
                pe.wait_ge(wkT_copied, i % 2 + 1)
                for j in range(4):
                    h = 2 * (4 * (i % 2) + j) + i // 2
                    at = slice(DH * (h % 2), DH * (h % 2) + DH)
                    blk = slice(P * (h // 2), P * (h // 2) + P)
                    t = pe.matmul(bank[:, P * j:P * (j + 1)], wqT[at, blk], wkT[at, blk],
                                  start=True, stop=True)
                t.then_inc(wqk_made, 1)

            def turn_x(src, half, done):
                for j in range(4):
                    t = pe.transpose((ps_o, ps_m)[half][:, 0, Q * j:Q * (j + 1)], src[0:Q, 4 * half + j, :],
                                     ident[0:Q, 0:Q])
                t.then_inc(done, 1)

            def make_pair(even, j, bank, x_two):
                for i in range(2):
                    t = pe.matmul(bank[:, 2 * Q * i:2 * Q * (i + 1)], wqk[:, head_cols(2 * j + i)], x_two,
                                  start=True, stop=True)
                t.then_inc(q_made, 1)

            turn_weights(0)
            for half in range(2):
                make_wqk(half)
                pe.wait_ge(xn_ready, 4 * (half + 1))
                turn_x(xn_rows, half, xn_turned)

            def turn_ctx(dst, c):
                j0 = TILE_SLOTS[c][0]
                for j in range(j0, min(j0 + 4, FULL)):
                    t = pe.transpose(dst[:, P * (j - j0):P * (j - j0 + 1)], ctx_raw[:, j, :], ident[:, :])
                if c == NC - 1:
                    t = pe.transpose(dst[:, P * (FULL - j0):P * (FULL - j0) + TAIL],
                                     ctx_raw[0:TAIL, FULL, :], ident[0:TAIL, 0:TAIL])
                return t

            pe.wait_ge(ctx_loaded, 64)
            for c in range(NC):
                turn_ctx(CTX0_BANKS[c], c).then_inc(ctx_turned, 1)
            pe.wait_ge(wqk_ready, 2)
            pe.wait_ge(xnT_copied, 1)
            make_pair(0, 0, PAIR0_BANK, xn_T[:, 0:2 * Q])
            for half in range(2):
                pe.wait_ge(xnT_copied, half + 1)
                turn_x(x_rows, half, x_turned)

            def window(pe, b, par, first, last, nxt):
                def scores(s, c):
                    if not item_exists(s, first, last):
                        return
                    item = ITEMS[s]
                    m = rows(item)
                    kind, k = item_event(b, s, NC, c)
                    before = score_before(s, c, first, last)
                    if before is not None:
                        k2, v2 = item_event(b, before[0], NC, before[1])
                        pe.wait_ge(exped[k2], v2)
                    if c == 0 and item == LATE:
                        pe.wait_ge(x1_hi_done, n(b - 1, 1, 0))
                    elif s == 0 and first:
                        pe.wait_ge(ctxT_lo, c + 1)
                        pe.wait_ge(q_lo_done, 1)
                    elif c == 0:
                        if s == 0:
                            pe.wait_ge(ctxT_lo, n(b, NC, NC - 1))
                        pair = min(HP, -(-(TM * item + m) // (2 * Q)))
                        pe.wait_ge(q_lo_done, pairs_up_to(b - par, pair - 1))
                    c0, w = CHUNKS[c]
                    cp = 1 - par if item == LATE else par
                    if item == LATE:
                        a_hi, a_lo = x1_hi[:, :], x1_lo[:, :]
                    else:
                        a_hi, a_lo = [q[:, par, TM * item:TM * item + m] for q in (q_hi, q_lo)]
                    dst = ps_s[0:m, score_bank(s, c, par), 0:w]
                    pe.matmul(dst, a_hi, cT_hi[cp][:, c0:c0 + w], start=True, stop=False)
                    pe.matmul(dst, a_hi, cT_lo[cp][:, c0:c0 + w], start=False, stop=False)
                    if c == 0 and item == LATE:
                        pe.wait_ge(x1_split, n(b - 1, 1, 0))
                    pe.matmul(dst, a_lo, cT_hi[cp][:, c0:c0 + w], start=False, stop=True)\
                        .then_inc(scored[kind], 1)

                def wait_bank(what, s, c):
                    before = turn_before(b, what, s, c, first, last, nxt)
                    if before is not None:
                        pe.wait_ge(*before)

                def turn(s, c):
                    if not ((s < 0 and not first) or (s >= 0 and item_exists(s, first, last))):
                        return
                    m = rows(ITEMS[s])
                    kind, k = item_event(b, s, NC, c)
                    pe.wait_ge(exped[kind], k)
                    wait_bank("item", s, c)
                    if first and s == 0 and c == 1:
                        pe.wait_ge(wqk_ready, 4)
                    bank = turn_bank("item", s, c, par)
                    j0, nj = TILE_SLOTS[c]
                    for j in range(j0, j0 + nj):
                        if j < FULL:
                            src = probs[s % 2][0:m, P * j:P * (j + 1)]
                        else:
                            kind2, k2 = item_event(b, s)
                            pe.wait_ge(tail_split[kind2], k2)
                            src = tails[s % 2][0:m, :]
                        t = pe.transpose(ps_t[:, bank, m * (j - j0):m * (j - j0 + 1)], src, ident[0:m, 0:m])
                    t.then_inc(turned[kind], 1)

                def passes(g, gb, cp):
                    w = Q if g == LATE else group_width(g)
                    col = LATE_COL if g == LATE else 0
                    buf = (NG * gb + (LATE_GROUP if g == LATE else g)) % 2
                    cols = slice(col, col + w)
                    whole, first_half = ps_o[:, 0, 0:2 * w].rearrange("p (a w) -> p a w", a=2), ps_o[:, 0, 0:w]
                    all_ = []
                    for j in range(FULL):
                        all_ += [(whole, c_hi[cp][:, j, :], pT_both[buf][:, j, :, cols]),
                                 (first_half, c_lo[cp][:, j, :], pT_both[buf][:, j, 0, cols])]
                    all_.append((first_half, c_hi[cp][:, FULL, :], pT_both[buf][:, FULL, 0, cols]))
                    return all_

                def pv(s, piece):
                    g, off, part, parts = PV_PLAN[s]
                    if (off < 0 and first) or (off >= 0 and last):
                        return
                    bb = b + off
                    par_b = (par + off) % 2
                    kind = "late" if g == LATE else "tile"
                    all_ = passes(g, par if g == LATE else par_b, par_b)
                    if part == 0 and piece == 0:
                        if g == LATE:
                            if not last:
                                pe.wait_ge(turned_lo["late"], n(bb, NC, NC - 1))
                            pe.wait_ge(pv_out["tile"], n(b, NG, LATE_GROUP - 1) if not last else n(b - 1, NG, NG - 1))
                        else:
                            if not (last and g == NG - 1):
                                pe.wait_ge(turned_lo["tile"], n(bb, NT * NC, GROUPS[g][-1] * NC + NC - 1))
                            if g == LATE_GROUP and not first:
                                pe.wait_ge(pv_out["late"], n(b - 1, 1, 0))
                            else:
                                need(pe, pv_out["tile"], n(bb, NG, g) - 1)
                            if g == 0 and first:
                                pe.wait_ge(wqk_ready, 3)
                            if g == 0:
                                pe.wait_ge(ctx_lo_done, n(bb, len(CTX_SPLIT), len(CTX_SPLIT) - 1))
                                pe.wait_ge(stack_steps, n(bb, 3, 2))
                    at = 2 * part + piece
                    lo, hi = PV_CUTS[parts][at:at + 2]
                    for i in range(lo, hi):
                        if last and g in (LATE, NG - 1) and i % 8 == 0:
                            if g == LATE:
                                pe.wait_ge(turned_lo["late"], n(bb, NC, i // 8))
                            else:
                                pe.wait_ge(turned_lo["tile"], n(bb, NT * NC, (NT - 1) * NC + i // 8))
                        t = pe.matmul(*all_[i],
                                      start=(i == 0), stop=(i == len(all_) - 1))
                    if part == parts - 1 and piece == 1:
                        t.then_inc(pv_done[kind], 1)

                def misc(s):
                    heads = (LAST_OUT_HEADS if last else OUT_HEADS).get(s)
                    if heads and not first:
                        if heads[0] == 0 and par == 1 and nxt:
                            pe.wait_ge(q_lo_done, pairs_up_to(b + 1, 0))
                        elif heads[0] == 0 and par == 0 and not last:
                            pe.wait_ge(q_lo_done, pairs_up_to(b, HP - 1))
                        group = group_of((Q * (heads[-1] + 1) - 1) // TM)
                        pe.wait_ge(o_normed, n(b - 1, NG, group))
                        for h in heads:
                            t = pe.matmul(ps_m[:, 0, 0:Q], wvo[:, head_cols(h)], o_norm[:, Q * h:Q * (h + 1)],
                                          start=(h == 0), stop=(h == H - 1))
                        if heads[-1] == H - 1:
                            t.then_inc(proj_made, 1)
                    if s == ROW_STEP and not first:
                        pe.wait_ge(x1_ready, n(b - 1, 1, 0))
                        if par == 1 and nxt:
                            pe.wait_ge(q_lo_done, pairs_up_to(b + 1, 5))
                        pe.transpose(ps_m[0:Q, 0, 0:D], x1_T[:, :], ident[:, :]).then_inc(x1_turned, 1)
                    if s == FIN_STEP and not first:
                        pe.wait_ge(pv_out["late"], n(b - 1, 1, 0))
                        pe.wait_ge(x1_rows_ready, n(b - 1, 1, 0))
                        pe.transpose(ps_m[0:Q, 0, 0:D], late_T[:, :], ident[:, :]).then_inc(fin_turned, 1)
                    if first and s == 0:
                        turn_weights(1)
                        pe.wait_ge(xT_copied, 2)
                    pair = pair_at(s, par, first, last, nxt)
                    if pair is not None:
                        j, off = pair
                        if j == 1 and not first:
                            pe.wait_ge(x1_ready, n(b - 1, 1, 0))
                        elif j == 6 and not first:
                            pe.wait_ge(fin_ready, n(b - 1, 1, 0))
                        elif j > 1:
                            pe.wait_ge(q_lo_done, pairs_up_to(b + off, j - 1))
                        if j == 0:
                            pe.wait_ge(xb_ready, b + 1)
                        if first and j == 4:
                            pe.wait_ge(wqk_ready, 4)
                        make_pair(b + off, j, ps_m[:, 0], xn_T[:, 0:2 * Q] if first else xb[:, :])
                    if first and s == 0:
                        make_wqk(2)
                        make_wqk(3)
                    if s == STEPS - 1 and pair is None and not last:
                        if first:
                            pe.wait_ge(wvo_ready, 4)
                        else:
                            pe.wait_ge(fin_ready, n(b - 1, 1, 0))
                    if first and s in WVT_STEPS:
                        i = WVT_STEPS[s]
                        if i == 0:
                            pe.wait_ge(wvo_loaded, 32)
                            pe.wait_ge(q_lo_done, HP)
                        else:
                            pe.wait_ge(wvT_copied, 1)
                        for j in range(4):
                            g = 4 * i + j
                            t = pe.transpose(ps_m[:, 0, P * j:P * (j + 1)], wv_sb[:, P * g:P * (g + 1)],
                                             ident[:, :])
                        t.then_inc(wvT_turned, 1)
                    if first and s in WVO_STEPS:
                        i = WVO_STEPS[s]
                        if i == 0:
                            pe.wait_ge(wvT_copied, 2)
                        else:
                            pe.wait_ge(wvo_ready, i)
                        for j in range(4):
                            h = 2 * (4 * (i % 2) + j) + i // 2
                            at = slice(DH * (h % 2), DH * (h % 2) + DH)
                            t = pe.matmul(ps_m[:, 0, P * j:P * (j + 1)], wvT[at, P * (h // 2):P * (h // 2) + P],
                                          wo_sb[at, h // 2, :], start=True, stop=True)
                        t.then_inc(wvo_made, 1)

                for s in range(STEPS):
                    scores(s, 0)
                    turn(s - 1, 0)
                    scores(s, 1)
                    turn(s - 1, 1)
                    scores(s, 2)
                    if last and s > 0:
                        turn(s - 1, 2)
                        pv_at = {LATE_AT + 1: PV_LAST[LATE, -1], PV_LAST[LATE, -1]: None}.get(s, s)
                        if pv_at is not None:
                            pv(pv_at, 0)
                            pv(pv_at, 1)
                        misc(s)
                    else:
                        pv(s, 0)
                        turn(s - 1, 2)
                        pv(s, 1)
                        misc(s)
                    if s in CTX_T_STEPS and nxt:
                        c = CTX_T_STEPS.index(s)
                        if c == 0:
                            pe.wait_ge(ctx_loaded, n(b + 1, 1, 0) * 64)
                        wait_bank("ctx", s, c)
                        turn_ctx(ps_t[:, turn_bank("ctx", s, c, par)], c).then_inc(ctx_turned, 1)

            windows(pe, window)


_INS = ['x', 'ctx_1024', 'L0_xattn_wq', 'L0_xattn_wk', 'L0_xattn_wv', 'L0_xattn_wo', 'L0_xattn_norm_w']
_OUTS = [((8, 100, 128), 'float32')]


def kernel(**inputs):
    import numpy as _np
    import concourse.bacc as _bacc
    from concourse import mybir as _mybir
    from concourse.bass_utils import run_bass_kernel_spmd as _run

    nc = _bacc.Bacc("TRN2", target_bir_lowering=False, num_devices=1)
    arrays, args = {}, []
    for name in _INS:
        a = _np.ascontiguousarray(inputs[name])
        arrays[f"in_{name}_dram"] = a
        args.append(nc.dram_tensor(f"in_{name}_dram", a.shape, _mybir.dt.from_np(a.dtype), kind="ExternalInput").ap())
    for i, (shape, dtype) in enumerate(_OUTS):
        dt = _mybir.dt.from_np(_np.dtype(dtype))
        args.append(nc.dram_tensor(f"out_{i}_dram", shape, dt, kind="ExternalOutput").ap())
    bass_two_cross_attentions(nc, *args)
    r = _run(nc, [arrays], core_ids=[0])
    return r.results[0]["out_0_dram"]
```
